# Optimizing a Trainium2 kernel written in Bass

```python
import numpy as np
import jax
import jax.numpy as jnp

def _softmax(x, axis=-1):
    return jax.nn.softmax(x, axis=axis)

def _gelu(x):
    return jax.nn.gelu(x, approximate=True)

def _silu(x):
    return jax.nn.silu(x)

def _sigmoid(x):
    return jax.nn.sigmoid(x)

def _layernorm(x, axis=-1, eps=1e-05):
    m = jnp.mean(x, axis=axis, keepdims=True)
    v = jnp.var(x, axis=axis, keepdims=True)
    return (x - m) / jnp.sqrt(v + eps)

def _scatter_add(tgt, idx, src, axis=0):
    return tgt.at[idx].add(src)

def _segment_sum(src, seg, n):
    return jax.ops.segment_sum(src, seg, n)
kernel_name = 'mk_decoder_postln_d2_seqx_r4_1e8736'

def setup_inputs(seed: int=0):
    np.random.seed(seed)
    _w = jnp.asarray

    def _rec_inputs():
        import jax
        import jax.numpy as jnp
        _rk = jax.random.key(seed)
        x = -0.0002928 + 1 * jax.random.normal(jax.random.fold_in(_rk, 1), (1, 2048, 256), jnp.float32)
        _lenS = 2048 - jax.random.randint(jax.random.fold_in(_rk, 7), (1,), 0, max(1, 2048 // 4) + 1, jnp.int32)
        _lenS2 = 1601 - jax.random.randint(jax.random.fold_in(_rk, 8), (1,), 0, max(1, 1601 // 4) + 1, jnp.int32)
        _ctx_1024P = jax.random.normal(jax.random.fold_in(_rk, 11), (1, 16, 256), jnp.float32)
        _ctx_1024c = jax.random.dirichlet(jax.random.fold_in(_rk, 511), 0.3 * jnp.ones((16,), jnp.float32), (1, 1601))
        _ctx_1024t = jnp.einsum('bsk,bkd->bsd', _ctx_1024c, _ctx_1024P)
        _ctx_1024t = _ctx_1024t * jax.lax.rsqrt(jnp.mean(jnp.square(_ctx_1024t)) + 1e-12) * 0.953939
        ctx_1024 = -1.39393e-06 + 0.999914 * (_ctx_1024t + 0.3 * jax.random.normal(jax.random.fold_in(_rk, 611), (1, 1601, 256), jnp.float32))
        _validS = jnp.arange(2048)[None, :] < _lenS[:, None]
        _validS2 = jnp.arange(1601)[None, :] < _lenS2[:, None]
        _causal = jnp.tril(jnp.ones((2048, 2048), dtype=bool))
        mask_BxS2_ik0 = jnp.where(jnp.broadcast_to(_validS2[:, :], (1, 1601)), 0, 1).astype(jnp.int32)
        return (x, ctx_1024, mask_BxS2_ik0)
    x, ctx_1024, mask_BxS2_ik0 = _rec_inputs()

    def _L0_attn_setup():
        import jax, jax.numpy as jnp
        import numpy as np
        LN_EPS = 1e-05
        WKV_EPS = 1e-08

        def _layernorm(x, g, b):
            mu = jnp.mean(x, axis=-1, keepdims=True)
            var = jnp.mean((x - mu) ** 2, axis=-1, keepdims=True)
            return (x - mu) * jax.lax.rsqrt(var + LN_EPS) * g + b

        def _time_mix(xn, Wr, Ww, Wk, Wv, Wo, time_decay):
            r = jax.nn.sigmoid(jnp.einsum('bsd,ed->bse', xn, Wr))
            w = -jnp.exp(jnp.einsum('bsd,ed->bse', xn, Ww))
            k = jnp.einsum('bsd,ed->bse', xn, Wk)
            v = jnp.einsum('bsd,ed->bse', xn, Wv)
            ewk = jnp.exp(w + k)
            decay = jnp.exp(time_decay)

            def step(carry, inp):
                num, den = carry
                e, vt = inp
                num = decay * num + e * vt
                den = decay * den + e
                wkv = num / (den + WKV_EPS)
                return ((num, den), wkv)
            B, S, D = xn.shape
            init = (jnp.zeros((B, D), xn.dtype), jnp.zeros((B, D), xn.dtype))
            (num_f, den_f), wkv = jax.lax.scan(step, init, (jnp.swapaxes(ewk, 0, 1), jnp.swapaxes(v, 0, 1)))
            wkv = jnp.swapaxes(wkv, 0, 1)
            out = jnp.einsum('bsd,ed->bse', r * wkv, Wo)
            final_state = jnp.stack([num_f, den_f], axis=1)
            return (out, final_state)

        def _channel_mix(xn, Wkey, Wval, Wrec):
            k = jnp.einsum('bsd,fd->bsf', xn, Wkey)
            k = jnp.square(jax.nn.relu(k))
            v = jnp.einsum('bsf,df->bsd', k, Wval)
            r = jax.nn.sigmoid(jnp.einsum('bsd,ed->bse', xn, Wrec))
            return r * v

        def _reference_tuple_inner(x, ln1_g, ln1_b, ln2_g, ln2_b, Wr, Ww, Wk, Wv, Wo, time_decay, time_first, Wkey, Wval, Wrec):
            tm, new_state = _time_mix(_layernorm(x, ln1_g, ln1_b), Wr, Ww, Wk, Wv, Wo, time_decay)
            x = x + tm
            x = x + _channel_mix(_layernorm(x, ln2_g, ln2_b), Wkey, Wval, Wrec)
            return (x, new_state)
        key = jax.random.key(seed)
        ks = jax.random.split(key, 16)
        B, S, D, F = (4, 512, 256, 1024)
        xavier_d = float(np.sqrt(6.0 / (D + D)))
        xavier_df = float(np.sqrt(6.0 / (D + F)))
        u = lambda k, sh, s: jax.random.uniform(k, sh, jnp.float32, -s, s)
        return {'x': jax.random.normal(ks[0], (B, S, D), jnp.float32), 'ln1_g': jnp.ones((D,), jnp.float32), 'ln1_b': jnp.zeros((D,), jnp.float32), 'ln2_g': jnp.ones((D,), jnp.float32), 'ln2_b': jnp.zeros((D,), jnp.float32), 'Wr': u(ks[1], (D, D), xavier_d), 'Ww': u(ks[2], (D, D), xavier_d), 'Wk': u(ks[3], (D, D), xavier_d), 'Wv': u(ks[4], (D, D), xavier_d), 'Wo': u(ks[5], (D, D), xavier_d), 'time_decay': jax.random.uniform(ks[6], (D,), jnp.float32, -1.0, 0.0), 'time_first': jax.random.uniform(ks[7], (D,), jnp.float32, -1.0, 1.0), 'Wkey': u(ks[8], (F, D), xavier_df), 'Wval': u(ks[9], (D, F), xavier_df), 'Wrec': u(ks[10], (D, D), xavier_d)}
    _L0_attn_all = _L0_attn_setup()
    _L0_attn_in = {k: v for k, v in _L0_attn_all.items() if k in ('ln1_g', 'ln1_b', 'ln2_g', 'ln2_b', 'Wr', 'Ww', 'Wk', 'Wv', 'Wo', 'time_decay', 'time_first', 'Wkey', 'Wval', 'Wrec')}
    del _L0_attn_all

    def _L0_xattn_setup():
        import jax, jax.numpy as jnp
        import numpy as np
        B, S, SE, D, H = (2, 512, 512, 256, 16)
        DH = D // H
        key = jax.random.key(seed)
        ks = jax.random.split(key, 6)
        scale = 0.02
        return {'hidden_states': jax.random.normal(ks[0], (B, S, D), dtype=jnp.float32), 'encoder_hidden_states': jax.random.normal(ks[1], (B, SE, D), dtype=jnp.float32), 'encoder_attention_mask': jax.random.randint(ks[2], (B, SE), 0, 2, dtype=jnp.int32), 'Wq': jax.random.normal(ks[3], (D, D), dtype=jnp.float32) * scale, 'Wkv': jax.random.normal(ks[4], (2 * D, D), dtype=jnp.float32) * scale, 'Wo': jax.random.normal(ks[5], (D, D), dtype=jnp.float32) * scale}
    _L0_xattn_all = _L0_xattn_setup()
    _L0_xattn_in = {k: v for k, v in _L0_xattn_all.items() if k in ('Wq', 'Wkv', 'Wo')}
    del _L0_xattn_all

    def _L0_ffn_setup():
        import jax, jax.numpy as jnp
        import numpy as np
        DIM = 256
        HIDDEN = 768
        SCALE = 1.0 / 127.0

        def _dequant(w_int, dtype):
            return w_int.astype(dtype) * jnp.asarray(SCALE, dtype)
        key = jax.random.key(seed)
        k_x, k_g, k_u, k_d = jax.random.split(key, 4)
        x = jax.random.normal(k_x, (4, 512, DIM), dtype=jnp.float32)
        w_gate = jax.random.randint(k_g, (HIDDEN, DIM), -127, 128, dtype=jnp.int32)
        w_up = jax.random.randint(k_u, (HIDDEN, DIM), -127, 128, dtype=jnp.int32)
        w_down = jax.random.randint(k_d, (DIM, HIDDEN), -127, 128, dtype=jnp.int32)
        return {'x': x, 'w_gate': w_gate, 'w_up': w_up, 'w_down': w_down}
    _L0_ffn_all = _L0_ffn_setup()
    _L0_ffn_in = {k: v for k, v in _L0_ffn_all.items() if k in ('w_gate', 'w_up', 'w_down')}
    del _L0_ffn_all

    def _L1_attn_setup():
        import jax, jax.numpy as jnp
        import numpy as np
        B, T, D = (4, 1024, 256)
        C = 8.0
        LOGIT_LO = float(np.log(0.9 / 0.1))
        LOGIT_HI = float(np.log(0.999 / 0.001))

        def rms_norm(x, g):
            n = jnp.maximum(jnp.linalg.norm(x, axis=-1, keepdims=True), 1e-12)
            return x / n * x.shape[-1] ** 0.5 * g

        def rg_lru(x, Wa, ba, Wx, bx, Lam):
            rt = jax.nn.sigmoid(jnp.einsum('btd,hd->bth', x, Wa) + ba)
            it = jax.nn.sigmoid(jnp.einsum('btd,hd->bth', x, Wx) + bx)
            log_a = -jax.nn.softplus(-Lam)
            a = jnp.exp(log_a * rt / C)
            gated = jnp.sqrt(1.0 - a * a) * (it * x)

            def step(h, ag):
                at, gt = ag
                h = at * h + gt
                return (h, h)
            h0 = jnp.zeros((x.shape[0], x.shape[2]), x.dtype)
            _, hs = jax.lax.scan(step, h0, (jnp.swapaxes(a, 0, 1), jnp.swapaxes(gated, 0, 1)))
            return jnp.swapaxes(hs, 0, 1)
        key = jax.random.key(seed)
        ks = jax.random.split(key, 12)
        s = 1.0 / np.sqrt(D)
        z = lambda: jnp.zeros((D,), jnp.float32)
        return {'x': jax.random.normal(ks[0], (B, T, D), jnp.float32), 'g1': jnp.ones((D,), jnp.float32), 'g2': jnp.ones((D,), jnp.float32), 'W_lin': jax.random.normal(ks[1], (D, D), jnp.float32) * s, 'b_lin': z(), 'W_conv': jax.random.normal(ks[2], (D, D), jnp.float32) * s, 'b_conv': z(), 'W_lin2': jax.random.normal(ks[3], (D, D), jnp.float32) * s, 'b_lin2': z(), 'Wa': jax.random.normal(ks[4], (D, D), jnp.float32) * s, 'ba': z(), 'Wx': jax.random.normal(ks[5], (D, D), jnp.float32) * s, 'bx': z(), 'Lam': jax.random.uniform(ks[6], (D,), jnp.float32, LOGIT_LO, LOGIT_HI), 'W1': jax.random.normal(ks[7], (D, D), jnp.float32) * s, 'b1': z(), 'W2': jax.random.normal(ks[8], (D, D), jnp.float32) * s, 'b2': z(), 'W3': jax.random.normal(ks[9], (D, D), jnp.float32) * s, 'b3': z()}
    _L1_attn_all = _L1_attn_setup()
    _L1_attn_in = {k: v for k, v in _L1_attn_all.items() if k in ('g1', 'g2', 'W_lin', 'b_lin', 'W_conv', 'b_conv', 'W_lin2', 'b_lin2', 'Wa', 'ba', 'Wx', 'bx', 'Lam', 'W1', 'b1', 'W2', 'b2', 'W3', 'b3')}
    del _L1_attn_all

    def _L1_xattn_setup():
        import jax, jax.numpy as jnp
        import numpy as np
        DIM = 256
        NUM_HEADS = 16
        HEAD_DIM = DIM // NUM_HEADS
        SCALE = HEAD_DIM ** (-0.5)
        key = jax.random.key(seed)
        k1, k2, k3, k4, k5, k6 = jax.random.split(key, 6)
        B, S, L = (4, 2048, 128)
        x = jax.random.normal(k1, (B, S, DIM), dtype=jnp.float32)
        latents = jax.random.normal(k2, (B, L, DIM), dtype=jnp.float32)
        w_q = jax.random.normal(k3, (DIM, DIM), dtype=jnp.float32) * DIM ** (-0.5)
        w_kv = jax.random.normal(k4, (2 * DIM, DIM), dtype=jnp.float32) * DIM ** (-0.5)
        w_out = jax.random.normal(k5, (DIM, DIM), dtype=jnp.float32) * DIM ** (-0.5)
        b_out = jax.random.normal(k6, (DIM,), dtype=jnp.float32) * 0.01
        return {'x': x, 'latents': latents, 'w_q': w_q, 'w_kv': w_kv, 'w_out': w_out, 'b_out': b_out}
    _L1_xattn_all = _L1_xattn_setup()
    _L1_xattn_in = {k: v for k, v in _L1_xattn_all.items() if k in ('w_q', 'w_kv', 'w_out', 'b_out')}
    del _L1_xattn_all

    def _L1_ffn_setup():
        import jax, jax.numpy as jnp
        import numpy as np
        TOP_K = 2
        key = jax.random.key(seed)
        k0, k1, k2, k3, k4 = jax.random.split(key, 5)
        B, S, H, I, E = (4, 512, 256, 704, 8)
        s_h = 1.0 / np.sqrt(H)
        s_i = 1.0 / np.sqrt(I)
        return {'x': jax.random.normal(k0, (B, S, H), jnp.float32), 'w_router': jax.random.normal(k1, (E, H), jnp.float32) * s_h, 'w_gate': jax.random.normal(k2, (E, I, H), jnp.float32) * s_h, 'w_up': jax.random.normal(k3, (E, I, H), jnp.float32) * s_h, 'w_down': jax.random.normal(k4, (E, H, I), jnp.float32) * s_i}
    _L1_ffn_all = _L1_ffn_setup()
    _L1_ffn_in = {k: v for k, v in _L1_ffn_all.items() if k in ('w_router', 'w_gate', 'w_up', 'w_down')}
    del _L1_ffn_all
    return {'x': x, 'ctx_1024': ctx_1024, 'mask_BxS2_ik0': mask_BxS2_ik0, 'L0_attn_ln1_g': _L0_attn_in['ln1_g'], 'L0_attn_ln1_b': _L0_attn_in['ln1_b'], 'L0_attn_ln2_g': _L0_attn_in['ln2_g'], 'L0_attn_ln2_b': _L0_attn_in['ln2_b'], 'L0_attn_Wr': _L0_attn_in['Wr'], 'L0_attn_Ww': _L0_attn_in['Ww'], 'L0_attn_Wk': _L0_attn_in['Wk'], 'L0_attn_Wv': _L0_attn_in['Wv'], 'L0_attn_Wo': _L0_attn_in['Wo'], 'L0_attn_time_decay': _L0_attn_in['time_decay'], 'L0_attn_time_first': _L0_attn_in['time_first'], 'L0_attn_Wkey': _L0_attn_in['Wkey'], 'L0_attn_Wval': _L0_attn_in['Wval'], 'L0_attn_Wrec': _L0_attn_in['Wrec'], 'L0_xattn_Wq': _L0_xattn_in['Wq'], 'L0_xattn_Wkv': _L0_xattn_in['Wkv'], 'L0_xattn_Wo': _L0_xattn_in['Wo'], 'L0_ffn_w_gate': _L0_ffn_in['w_gate'], 'L0_ffn_w_up': _L0_ffn_in['w_up'], 'L0_ffn_w_down': _L0_ffn_in['w_down'], 'L1_attn_g1': _L1_attn_in['g1'], 'L1_attn_g2': _L1_attn_in['g2'], 'L1_attn_W_lin': _L1_attn_in['W_lin'], 'L1_attn_b_lin': _L1_attn_in['b_lin'], 'L1_attn_W_conv': _L1_attn_in['W_conv'], 'L1_attn_b_conv': _L1_attn_in['b_conv'], 'L1_attn_W_lin2': _L1_attn_in['W_lin2'], 'L1_attn_b_lin2': _L1_attn_in['b_lin2'], 'L1_attn_Wa': _L1_attn_in['Wa'], 'L1_attn_ba': _L1_attn_in['ba'], 'L1_attn_Wx': _L1_attn_in['Wx'], 'L1_attn_bx': _L1_attn_in['bx'], 'L1_attn_Lam': _L1_attn_in['Lam'], 'L1_attn_W1': _L1_attn_in['W1'], 'L1_attn_b1': _L1_attn_in['b1'], 'L1_attn_W2': _L1_attn_in['W2'], 'L1_attn_b2': _L1_attn_in['b2'], 'L1_attn_W3': _L1_attn_in['W3'], 'L1_attn_b3': _L1_attn_in['b3'], 'L1_xattn_w_q': _L1_xattn_in['w_q'], 'L1_xattn_w_kv': _L1_xattn_in['w_kv'], 'L1_xattn_w_out': _L1_xattn_in['w_out'], 'L1_xattn_b_out': _L1_xattn_in['b_out'], 'L1_ffn_w_router': _L1_ffn_in['w_router'], 'L1_ffn_w_gate': _L1_ffn_in['w_gate'], 'L1_ffn_w_up': _L1_ffn_in['w_up'], 'L1_ffn_w_down': _L1_ffn_in['w_down']}

def reference(x, ctx_1024, mask_BxS2_ik0, L0_attn_ln1_g, L0_attn_ln1_b, L0_attn_ln2_g, L0_attn_ln2_b, L0_attn_Wr, L0_attn_Ww, L0_attn_Wk, L0_attn_Wv, L0_attn_Wo, L0_attn_time_decay, L0_attn_time_first, L0_attn_Wkey, L0_attn_Wval, L0_attn_Wrec, L0_xattn_Wq, L0_xattn_Wkv, L0_xattn_Wo, L0_ffn_w_gate, L0_ffn_w_up, L0_ffn_w_down, L1_attn_g1, L1_attn_g2, L1_attn_W_lin, L1_attn_b_lin, L1_attn_W_conv, L1_attn_b_conv, L1_attn_W_lin2, L1_attn_b_lin2, L1_attn_Wa, L1_attn_ba, L1_attn_Wx, L1_attn_bx, L1_attn_Lam, L1_attn_W1, L1_attn_b1, L1_attn_W2, L1_attn_b2, L1_attn_W3, L1_attn_b3, L1_xattn_w_q, L1_xattn_w_kv, L1_xattn_w_out, L1_xattn_b_out, L1_ffn_w_router, L1_ffn_w_gate, L1_ffn_w_up, L1_ffn_w_down):
    import jax
    import jax.numpy as jnp

    def _L0_attn_ref(x, ln1_g, ln1_b, ln2_g, ln2_b, Wr, Ww, Wk, Wv, Wo, time_decay, time_first, Wkey, Wval, Wrec):
        import jax, jax.numpy as jnp
        import numpy as np
        LN_EPS = 1e-05
        WKV_EPS = 1e-08

        def _layernorm(x, g, b):
            mu = jnp.mean(x, axis=-1, keepdims=True)
            var = jnp.mean((x - mu) ** 2, axis=-1, keepdims=True)
            return (x - mu) * jax.lax.rsqrt(var + LN_EPS) * g + b

        def _time_mix(xn, Wr, Ww, Wk, Wv, Wo, time_decay):
            r = jax.nn.sigmoid(jnp.einsum('bsd,ed->bse', xn, Wr))
            w = -jnp.exp(jnp.einsum('bsd,ed->bse', xn, Ww))
            k = jnp.einsum('bsd,ed->bse', xn, Wk)
            v = jnp.einsum('bsd,ed->bse', xn, Wv)
            ewk = jnp.exp(w + k)
            decay = jnp.exp(time_decay)

            def step(carry, inp):
                num, den = carry
                e, vt = inp
                num = decay * num + e * vt
                den = decay * den + e
                wkv = num / (den + WKV_EPS)
                return ((num, den), wkv)
            B, S, D = xn.shape
            init = (jnp.zeros((B, D), xn.dtype), jnp.zeros((B, D), xn.dtype))
            (num_f, den_f), wkv = jax.lax.scan(step, init, (jnp.swapaxes(ewk, 0, 1), jnp.swapaxes(v, 0, 1)))
            wkv = jnp.swapaxes(wkv, 0, 1)
            out = jnp.einsum('bsd,ed->bse', r * wkv, Wo)
            final_state = jnp.stack([num_f, den_f], axis=1)
            return (out, final_state)

        def _channel_mix(xn, Wkey, Wval, Wrec):
            k = jnp.einsum('bsd,fd->bsf', xn, Wkey)
            k = jnp.square(jax.nn.relu(k))
            v = jnp.einsum('bsf,df->bsd', k, Wval)
            r = jax.nn.sigmoid(jnp.einsum('bsd,ed->bse', xn, Wrec))
            return r * v

        def _reference_tuple_inner(x, ln1_g, ln1_b, ln2_g, ln2_b, Wr, Ww, Wk, Wv, Wo, time_decay, time_first, Wkey, Wval, Wrec):
            tm, new_state = _time_mix(_layernorm(x, ln1_g, ln1_b), Wr, Ww, Wk, Wv, Wo, time_decay)
            x = x + tm
            x = x + _channel_mix(_layernorm(x, ln2_g, ln2_b), Wkey, Wval, Wrec)
            return (x, new_state)
        return _reference_tuple_inner(x, ln1_g, ln1_b, ln2_g, ln2_b, Wr, Ww, Wk, Wv, Wo, time_decay, time_first, Wkey, Wval, Wrec)[0]

    def _L0_xattn_ref(hidden_states, encoder_hidden_states, encoder_attention_mask, Wq, Wkv, Wo):
        import jax, jax.numpy as jnp
        import numpy as np
        B, S, SE, D, H = (2, 512, 512, 256, 16)
        DH = D // H
        b, s, _ = hidden_states.shape
        se = encoder_hidden_states.shape[1]
        att_scale = DH ** (-0.5)
        q = (hidden_states @ Wq.T).reshape(b, s, H, DH).transpose(0, 2, 1, 3)
        kv = (encoder_hidden_states @ Wkv.T).reshape(b, se, 2, H, DH).transpose(2, 0, 3, 1, 4)
        k, v = (kv[0], kv[1])
        scores = jnp.einsum('bhsd,bhed->bhse', q, k) * att_scale
        mask = encoder_attention_mask[:, None, None, :]
        scores = jnp.where(mask == 0, -jnp.inf, scores)
        attn = jax.nn.softmax(scores, axis=-1)
        out = jnp.einsum('bhse,bhed->bhsd', attn, v)
        out = out.transpose(0, 2, 1, 3).reshape(b, s, H * DH)
        return out @ Wo.T

    def _L0_ffn_ref(x, w_gate, w_up, w_down):
        import jax, jax.numpy as jnp
        import numpy as np
        DIM = 256
        HIDDEN = 768
        SCALE = 1.0 / 127.0

        def _dequant(w_int, dtype):
            return w_int.astype(dtype) * jnp.asarray(SCALE, dtype)
        wg = _dequant(w_gate, x.dtype)
        wu = _dequant(w_up, x.dtype)
        wd = _dequant(w_down, x.dtype)
        gate = jnp.einsum('bsd,hd->bsh', x, wg)
        up = jnp.einsum('bsd,hd->bsh', x, wu)
        h = jax.nn.silu(gate) * up
        return jnp.einsum('bsh,dh->bsd', h, wd)

    def _L1_attn_ref(x, g1, g2, W_lin, b_lin, W_conv, b_conv, W_lin2, b_lin2, Wa, ba, Wx, bx, Lam, W1, b1, W2, b2, W3, b3):
        import jax, jax.numpy as jnp
        import numpy as np
        B, T, D = (4, 1024, 256)
        C = 8.0
        LOGIT_LO = float(np.log(0.9 / 0.1))
        LOGIT_HI = float(np.log(0.999 / 0.001))

        def rms_norm(x, g):
            n = jnp.maximum(jnp.linalg.norm(x, axis=-1, keepdims=True), 1e-12)
            return x / n * x.shape[-1] ** 0.5 * g

        def rg_lru(x, Wa, ba, Wx, bx, Lam):
            rt = jax.nn.sigmoid(jnp.einsum('btd,hd->bth', x, Wa) + ba)
            it = jax.nn.sigmoid(jnp.einsum('btd,hd->bth', x, Wx) + bx)
            log_a = -jax.nn.softplus(-Lam)
            a = jnp.exp(log_a * rt / C)
            gated = jnp.sqrt(1.0 - a * a) * (it * x)

            def step(h, ag):
                at, gt = ag
                h = at * h + gt
                return (h, h)
            h0 = jnp.zeros((x.shape[0], x.shape[2]), x.dtype)
            _, hs = jax.lax.scan(step, h0, (jnp.swapaxes(a, 0, 1), jnp.swapaxes(gated, 0, 1)))
            return jnp.swapaxes(hs, 0, 1)
        residual = x
        xn = rms_norm(x, g1)
        lin = xn @ W_lin.T + b_lin
        x_gel = jax.nn.gelu(lin, approximate=False)
        x_rg = lin @ W_conv.T + b_conv
        x_rg = rg_lru(x_rg, Wa, ba, Wx, bx, Lam)
        xr = x_gel * x_rg @ W_lin2.T + b_lin2
        residual = xr + residual
        xm = rms_norm(residual, g2)
        out = jax.nn.sigmoid(xm @ W1.T + b1)
        gate = jax.nn.gelu(out, approximate=False)
        combined = gate * (xm @ W2.T + b2)
        y = combined @ W3.T + b3
        return y + residual

    def _L1_xattn_ref(x, latents, w_q, w_kv, w_out, b_out):
        import jax, jax.numpy as jnp
        import numpy as np
        DIM = 256
        NUM_HEADS = 16
        HEAD_DIM = DIM // NUM_HEADS
        SCALE = HEAD_DIM ** (-0.5)
        B, L, _ = latents.shape
        S = x.shape[1]
        q = latents @ w_q.T
        kv = x @ w_kv.T
        k, v = jnp.split(kv, 2, axis=-1)
        q = q.reshape(B, L, NUM_HEADS, HEAD_DIM)
        k = k.reshape(B, S, NUM_HEADS, HEAD_DIM)
        v = v.reshape(B, S, NUM_HEADS, HEAD_DIM)
        attn = jnp.einsum('blhd,bshd->bhls', q, k) * SCALE
        attn = jax.nn.softmax(attn, axis=-1)
        out = jnp.einsum('bhls,bshd->blhd', attn, v)
        out = out.reshape(B, L, DIM)
        return out @ w_out.T + b_out

    def _L1_ffn_ref(x, w_router, w_gate, w_up, w_down):
        import jax, jax.numpy as jnp
        import numpy as np
        TOP_K = 2
        B, S, H = x.shape
        E = w_router.shape[0]
        xf = x.reshape(-1, H)
        logits = jnp.einsum('th,eh->te', xf, w_router)
        probs = jax.nn.softmax(logits, axis=-1)
        topw, topi = jax.lax.top_k(probs, TOP_K)
        topw = topw / jnp.sum(topw, axis=-1, keepdims=True)
        onehot = (topi[..., None] == jnp.arange(E)).astype(x.dtype)
        combine = jnp.einsum('tk,tke->te', topw, onehot)
        gate = jax.nn.silu(jnp.einsum('th,eih->eti', xf, w_gate))
        up = jnp.einsum('th,eih->eti', xf, w_up)
        down = jnp.einsum('eti,ehi->eth', gate * up, w_down)
        out = jnp.einsum('eth,te->th', down, combine)
        return out.reshape(B, S, H)
    x = _layernorm(x + _L0_attn_ref(x, L0_attn_ln1_g, L0_attn_ln1_b, L0_attn_ln2_g, L0_attn_ln2_b, L0_attn_Wr, L0_attn_Ww, L0_attn_Wk, L0_attn_Wv, L0_attn_Wo, L0_attn_time_decay, L0_attn_time_first, L0_attn_Wkey, L0_attn_Wval, L0_attn_Wrec), axis=-1)
    x = _layernorm(x + _L0_xattn_ref(x, ctx_1024, mask_BxS2_ik0, L0_xattn_Wq, L0_xattn_Wkv, L0_xattn_Wo), axis=-1)
    x = _layernorm(x + _L0_ffn_ref(x, L0_ffn_w_gate, L0_ffn_w_up, L0_ffn_w_down), axis=-1)
    x = _layernorm(x + _L1_attn_ref(x, L1_attn_g1, L1_attn_g2, L1_attn_W_lin, L1_attn_b_lin, L1_attn_W_conv, L1_attn_b_conv, L1_attn_W_lin2, L1_attn_b_lin2, L1_attn_Wa, L1_attn_ba, L1_attn_Wx, L1_attn_bx, L1_attn_Lam, L1_attn_W1, L1_attn_b1, L1_attn_W2, L1_attn_b2, L1_attn_W3, L1_attn_b3), axis=-1)
    x = _layernorm(x + _L1_xattn_ref(ctx_1024, x, L1_xattn_w_q, L1_xattn_w_kv, L1_xattn_w_out, L1_xattn_b_out), axis=-1)
    x = _layernorm(x + _L1_ffn_ref(x, L1_ffn_w_router, L1_ffn_w_gate, L1_ffn_w_up, L1_ffn_w_down), axis=-1)
    return x

_drawn_inputs = setup_inputs


def setup_inputs(seed=0):
    import zlib

    import numpy as np

    out = dict(_drawn_inputs(seed))
    spreads = {'L0_attn_ln1_g': (1.0, 0.2),
     'L0_attn_ln1_b': (0.0, 0.1),
     'L0_attn_ln2_g': (1.0, 0.2),
     'L0_attn_ln2_b': (0.0, 0.1),
     'L1_attn_g1': (1.0, 0.2),
     'L1_attn_g2': (1.0, 0.2),
     'L1_attn_b_lin': (0.0, 0.1),
     'L1_attn_b_conv': (0.0, 0.1),
     'L1_attn_b_lin2': (0.0, 0.1),
     'L1_attn_ba': (0.0, 0.329),
     'L1_attn_bx': (0.0, 0.1),
     'L1_attn_b1': (0.0, 0.351),
     'L1_attn_b2': (0.0, 0.1),
     'L1_attn_b3': (0.0, 0.1)}
    factors = {'L0_xattn_Wq': 4.446}
    for name, (base, spread) in spreads.items():
        noise = np.random.default_rng([zlib.crc32(name.encode()), seed]).standard_normal(out[name].shape)
        drawn = base * np.exp(spread * noise) if base else spread * noise
        out[name] = jnp.asarray(drawn.astype(out[name].dtype))
    for name, factor in factors.items():
        out[name] = (out[name] * factor).astype(out[name].dtype)
    return out
```

```python
from contextlib import ExitStack

import numpy as np

import concourse.bass as bass
from concourse import mybir

ALU = mybir.AluOpType
ACT = mybir.ActivationFunctionType
AX = mybir.AxisListType
F32 = mybir.dt.float32
BF16 = mybir.dt.bfloat16
I32 = mybir.dt.int32
U32 = mybir.dt.uint32

P = 128
T = 2048
D = 256
HALVES = D // P
CH = 512
NC = T // CH
S = 1601
NKT = -(-S // P)
WINDOW = 4
WINDOW_STEPS = 10
SP = NKT * P
H, DH = 16, 16
HG = 4
G = H // HG
F0 = 1024
F1 = 768
NE, FE = 8, 704
FT = -(-FE // P)
HALF = FE // 2
TILES = 2 * T // P + NE
QT = CH // P
NT = T // P
LN_EPS, WKV_EPS = 1e-5, 1e-8
MASKED = -1e30
DEQUANT = 1.0 / 127.0
N_CONST = 8
ARENA = 53208
ROWS = 100
RMS_SCALE = 2.0 ** 26
Q_PART = (0, 0, 1, 0, 2, 1)
K_PART = (0, 1, 0, 2, 0, 1)

LN_EXP, SIGMOID, SILU, GELU, SQRT = ("natural_log_exp_and_others", "sigmoid_and_others", "silu_and_others",
                                     "gelu_and_others", "sqrt_and_others")

VECS = ["ln1_g", "ln1_b", "ln2_g", "ln2_b", "time_decay", "g1", "g2", "b_lin", "b_conv", "b_lin2", "ba", "bx",
        "Lam", "b1", "b2", "b3", "b_out"]

W_RWKV = [("Wr", 2, D), ("Ww", 2, D), ("Wk", 2, D), ("Wv", 2, D), ("Wo", 2, D), ("Wrec", 2, D),
          ("Wkey", 2, F0), ("Wval", F0 // P, D)]
W_XATT = [("Wq", 2, D), ("WK", 2, D), ("WV", 2, D)]
W_INT = [("gate", 2, F1), ("up", 2, F1), ("down", F1 // P, D)]
W_LRU = [("W_lin", 2, D), ("W_conv", 2, D), ("Wa", 2, D), ("Wx", 2, D), ("W_lin2", 2, D), ("W1", 2, D),
         ("W2", 2, D), ("W3", 2, D)]


def width(group):
    return sum(k * n for _, k, n in group)


def views(ap, group):
    out, at = {}, 0
    for name, k, n in group:
        out[name] = ap[:, at:at + k * n].rearrange("p (k n) -> p k n", k=k)
        at += k * n
    return out


class Stage:

    def __init__(self, sem, per, base=0):
        self.sem, self.per, self.base = sem, per, base

    def again(self):
        return Stage(self.sem, self.per, self.base + self.per * NC)

    def wait(self, eng, chunk, part=None):
        eng.wait_ge(self.sem, self.per * chunk + (self.base + (self.per if part is None else part)))

    def wait_all(self, eng):
        eng.wait_ge(self.sem, self.base + self.per * NC)


class Count:

    def __init__(self, sem, base):
        self.sem, self.base = sem, base

    def wait(self, eng, n):
        eng.wait_ge(self.sem, n + self.base)


def tok(c, n=CH):
    return bass.ds(c * n, n)


def decoder(nc, io):
    with ExitStack() as ctx:
        def sem(name):
            return ctx.enter_context(nc.semaphore(name))

        parts_of = {"sync": [], "pool": [], "pe": [], "dve": [], "act": []}

        def stage(name, per=1, primed=None):
            st = Stage(sem(name), per, 1 if primed else 0)
            if primed:
                parts_of[primed].append(lambda eng: eng.sem_inc(st.sem, 1))
            return st

        arena = ctx.enter_context(nc.sbuf_tensor("arena", [P, ARENA], F32))
        ps = ctx.enter_context(nc.psum_tensor("ps", [P, 8, 512], F32))
        kparts = nc.dram_tensor("kparts", (3, D, SP), BF16, kind="Internal")
        mask_rows = nc.dram_tensor("mask_rows", (1, SP), BF16, kind="Internal")
        qparts = nc.dram_tensor("qparts", (3, D, T), BF16, kind="Internal")

        at = [0]

        def area(words):
            at[0] += words
            return at[0] - words

        def f32(start, *shape):
            n = int(np.prod(shape))
            v = arena[:, start:start + n]
            names = "abcd"[:len(shape)]
            if len(shape) == 1:
                return v
            return v.rearrange(f"p ({' '.join(names)}) -> p {' '.join(names)}",
                               **{k: s for k, s in zip(names[1:], shape[1:])})

        def bf16(start, *shape):
            n = int(np.prod(shape))
            v = arena[:, start:start + n // 2].bitcast(BF16)
            names = "abcd"[:len(shape)]
            if len(shape) == 1:
                return v
            return v.rearrange(f"p ({' '.join(names)}) -> p {' '.join(names)}",
                               **{k: s for k, s in zip(names[1:], shape[1:])})

        X = f32(area(2 * T), 2, T)
        ident = f32(area(P), P)
        mean_w = f32(area(P), P)
        pick_den = f32(area(P), P)
        vecs = f32(area(2 * len(VECS)), len(VECS), 2)
        vec = {n: vecs[:, i, :] for i, n in enumerate(VECS)}
        decay = f32(area(2), 2)
        rate = f32(area(2), 2)
        tmp2 = f32(area(4), 2, 2)
        eps_col = f32(area(1), 1)
        wkv_eps_col = f32(area(1), 1)
        one_col = f32(area(1), 1)
        zero_col = f32(area(1), 1)
        pad_keep = f32(area(NKT), NKT)
        mask_i = f32(area(NKT), NKT).bitcast(I32)
        keep = f32(area(2 * NKT), 2, NKT)
        counting = f32(area(16), 16)
        experts = counting[:, 0:NE]
        window_keep = f32(area(WINDOW), WINDOW)
        window_f = f32(ARENA - 64, NKT * 3 + 4)
        window_at = f32(area(4), 4).bitcast(I32)
        router = f32(area(2 * NE), 2, NE)

        WA = area(width(W_RWKV))
        WB = area(width(W_XATT) + G * D + width(W_INT))
        work = at[0]
        rwkv = views(f32(WA, width(W_RWKV)), W_RWKV)
        xatt = [views(f32(WB, width(W_XATT)), W_XATT), None]
        out_w = [f32(WB + width(W_XATT), G, D), None]
        ffn_at = WB + width(W_XATT) + G * D
        ffn = views(f32(ffn_at, width(W_INT)), W_INT)
        ffn_flat = f32(ffn_at, width(W_INT))
        ffn_int_flat = ffn_flat.bitcast(I32)
        lru = views(f32(WA, width(W_LRU)), W_LRU)
        xatt1_at = WA + width(W_LRU)
        xatt[1] = views(f32(xatt1_at, width(W_XATT)), W_XATT)
        out_w[1] = f32(xatt1_at + width(W_XATT), G, D)
        assert width(W_LRU) + width(W_XATT) + G * D <= width(W_RWKV)

        BUF = 2 * T
        XN, XC, SQ, B1, B2, B3, B4, B5 = (f32(work + i * BUF, 2, T) for i in range(8))
        a0 = work
        Kst = bf16(a0, H, SP)
        a0 += H * SP // 2
        Vaug = f32(a0, NKT, H, 32)
        a0 += NKT * H * 32
        Qst = bf16(a0, 4, HG, CH)
        a0 += 4 * HG * CH // 2
        probs = f32(a0, 2, HG, CH)
        ctxT = f32(a0, 2, SP)
        a0 += 2 * HG * CH
        On = f32(a0, HG, CH)
        parts = bf16(a0, 2, 3, 2, CH)
        a0 += G * CH
        Osb = f32(a0, 2, CH)
        a0 += 2 * CH
        Rden = f32(a0, 2, CH)
        rest = f32(a0, 2, CH)
        a0 += 2 * CH
        MX = f32(a0, 2, 16, 2)
        a0 += 64
        Mneg = f32(a0, 2, 16)
        a0 += 32
        Mres = f32(a0, P)
        a0 += P
        Mp = bf16(a0, 2, 3, P)
        a0 += 3 * P
        assert max(a0, work + 8 * BUF) <= ARENA, a0
        norm_sum, norm_rstd = B5[:, 0, :], B5[:, 1, :]
        mask_row_i = f32(work + 6 * BUF, SP).bitcast(I32)
        mask_row = bf16(work + 6 * BUF + SP, SP)
        EW = 2 * FE + 2 * FE + FT * D
        experts_all = f32(WA, NE * EW)
        FIRST_EXPERTS = (work + BUF - WA) // EW
        e0 = [WA + NE * EW]

        def place_of(*shape):
            e0[0] += int(np.prod(shape))
            assert e0[0] <= ARENA, e0
            return f32(e0[0] - int(np.prod(shape)), *shape)

        acc = place_of(NT, D)
        upper, scan_keep, row_start = place_of(P), place_of(NE * NT), place_of(TILES)
        assert e0[0] <= work + 7 * BUF
        logits, top, top_f, chosen, where = (place_of(NT, NE) for _ in range(5))
        top_i = place_of(NT, NE).bitcast(U32)
        is_top = place_of(2, NT, NE)
        count_in, count_to, over = (place_of(NE, NT) for _ in range(3))
        e_rows, e_end = place_of(NE), place_of(NE)
        place_f, place = place_of(2, NT), place_of(2, NT).bitcast(U32)
        ended, tile_expert_f = place_of(TILES, NE), place_of(TILES)
        tile_expert = place_of(TILES).bitcast(I32)
        wts, stats, aggr, std = place_of(4, NT), place_of(NT, 6), place_of(NT, 2), place_of(2, NT)
        rows, rowsT, h_rows = place_of(2, D), place_of(2, 2, P), place_of(2, FE)
        hiddenT, silu, y = place_of(FT, P), place_of(2, HALF), place_of(2, D)
        back = f32(WA, 2, NT, D)
        rows_in = nc.dram_tensor("rows_in", (TILES * P, D), F32, kind="Internal")
        rows_out = nc.dram_tensor("rows_out", (TILES * P, D), F32, kind="Internal")

        ld_x = [sem(f"ld_x{i}") for i in range(NC)]
        ld_const = sem("ld_const")
        ld_rwkv = [sem("ld_rwkv0"), sem("ld_rwkv1")]
        ld_xw = [sem("ld_xw0"), sem("ld_xw1")]
        ld_ffn = sem("ld_ffn")
        ld_lru = sem("ld_lru")
        ld_mean, rows_cleared = sem("ld_mean"), sem("rows_in_cleared")
        cols_set, consts_set, consts_dve = sem("bias_columns_set"), sem("out_weights_cleared"), sem("keep_and_rate")
        act_const = sem("decay_and_rate_logs")
        window_steps, window_kept = sem("window_steps"), sem("window_kept")
        mask_row_done, mask_row_out = sem("mask_row_done"), sem("mask_row_out")

        P_FIRST = 4 * 2 * D

        def part(engine):
            def add(f):
                parts_of[engine].append(f)
                return f
            return add

        def bank(c, n=1):
            return ps[:, bass.ds(c, n), :]

        def both(row):
            return row.unsqueeze(1).broadcast_to([P, 2, CH])

        @part("sync")
        def _(eng):
            for c in range(NC):
                eng.dma_start(X[:, :, tok(c)], io["xT"][:, :, tok(c)]).then_inc(ld_x[c], 16)
                if c == 0:
                    eng.dma_start(mean_w, io["mean_w"][:]).then_inc(ld_mean, 16)
            for dst, name in ((vecs, "vecs"), (ident, "ident"), (pick_den, "pick_den"), (pad_keep, "pad_keep"),
                              (counting, "counting"), (router, "router"), (mask_i, "mask_col")):
                eng.dma_start(dst, io[name][:]).then_inc(ld_const, 16)
            eng.dma_start(mask_row_i[0:1, :], io["mask_row"][:]).then_inc(ld_const, 16)
            eng.dma_start(f32(WA, P_FIRST), io["w_rwkv"][:, 0:P_FIRST]).then_inc(ld_rwkv[0], 16)
            eng.dma_start(f32(WA + P_FIRST, width(W_RWKV) - P_FIRST),
                          io["w_rwkv"][:, P_FIRST:]).then_inc(ld_rwkv[1], 16)
            eng.dma_start(f32(WB, width(W_XATT)), io["w_xatt0"][:]).then_inc(ld_xw[0], 16)
            eng.dma_start(ffn_int_flat, io["w_ffn"][:]).then_inc(ld_ffn, 16)
            eng.wait_ge(consts_set, 1)
            eng.dma_start(rows_in.rearrange("(j p) d -> p j d", p=P),
                          out_w[0][:, 0:1, :].broadcast_to([P, TILES, D])).then_inc(rows_cleared, 16)
            eng.wait_ge(rows_cleared, 16)
            for j in range(HG):
                eng.dma_start(out_w[0][32 * j:32 * j + DH, :, :],
                              io["w_out0"][:, j, :, :].rearrange("g i n -> i g n")).then_inc(ld_xw[0], 16)
            eng.wait_ge(mask_row_done, 1)
            eng.dma_start(mask_rows[:], mask_row[0:1, :]).then_inc(mask_row_out, 16)

        @part("pool")
        def _(eng):
            for col, value in ((eps_col, LN_EPS), (wkv_eps_col, WKV_EPS), (one_col, 1.0), (zero_col, 0.0)):
                eng.memset(col, value).then_inc(cols_set, 1)
            eng.memset(out_w[0], 0.0).then_inc(consts_set, 1)

        @part("dve")
        def _(eng):
            eng.wait_ge(ld_const, 16 * N_CONST)
            eng.tensor_scalar(keep[:, 0, :], mask_i, 0, None, ALU.not_equal).then_inc(consts_dve, 1)
            eng.tensor_copy(keep[:, 1, :], pad_keep).then_inc(consts_dve, 1)
            eng.tensor_scalar(mask_row[0:1, :], mask_row_i[0:1, :], 0, MASKED, ALU.is_equal,
                              ALU.mult).then_inc(mask_row_done, 1)
            steps = [0]

            def link(ins):
                steps[0] += 1
                ins.then_inc(window_steps, 1)
                eng.wait_ge(window_steps, steps[0])

            eng.wait_ge(mask_row_done, 1)
            best, less, more = (window_f[0:1, i * NKT:(i + 1) * NKT] for i in range(3))
            ends = window_f[0:1, 3 * NKT:3 * NKT + 4]
            link(eng.tensor_reduce(best, mask_row[0:1, :].rearrange("o (t k) -> o t k", k=P), AX.X, ALU.max))
            link(eng.tensor_tensor(less, best, counting[0:1, 0:NKT], ALU.subtract))
            link(eng.tensor_tensor(more, best, counting[0:1, 0:NKT], ALU.add))
            link(eng.tensor_reduce(ends[:, 0:1], less, AX.X, ALU.max))
            link(eng.tensor_reduce(ends[:, 1:2], more, AX.X, ALU.max))
            link(eng.tensor_scalar(ends[:, 0:1], ends[:, 0:1], -1.0, float(NKT - WINDOW), ALU.mult, ALU.min))
            link(eng.tensor_tensor(ends[:, 2:3], ends[:, 1:2], ends[:, 0:1], ALU.subtract))
            link(eng.tensor_copy(window_at[0:1, 0:1], ends[:, 0:1]))
            link(eng.tensor_scalar(window_at[0:1, 1:2], ends[:, 0:1], float(P), None, ALU.mult))
            link(eng.tensor_scalar(window_at[0:1, 2:3], ends[:, 2:3], float(WINDOW), None, ALU.is_lt))
            assert steps[0] == WINDOW_STEPS

        @part("act")
        def _(eng):
            eng.wait_ge(cols_set, 4)
            eng.wait_ge(ld_const, 16 * N_CONST)
            eng.activation(decay, vec["time_decay"], ACT.Exp, bias=zero_col).then_inc(act_const, 1)
            eng.activation(tmp2[:, 0, :], vec["Lam"], ACT.Abs).then_inc(act_const, 1)
            eng.wait_ge(act_const, 2)
            eng.activation(tmp2[:, 0, :], tmp2[:, 0, :], ACT.Exp, bias=zero_col, scale=-1.0).then_inc(act_const, 1)
            eng.wait_ge(act_const, 3)
            eng.activation(tmp2[:, 0, :], tmp2[:, 0, :], ACT.Ln, bias=one_col).then_inc(act_const, 1)

        @part("dve")
        def _(eng):
            eng.tensor_scalar(tmp2[:, 1, :], vec["Lam"], 0.0, None, ALU.min).then_inc(consts_dve, 1)
            eng.wait_ge(consts_dve, 3)
            eng.wait_ge(act_const, 4)
            eng.tensor_tensor(rate, tmp2[:, 1, :], tmp2[:, 0, :], ALU.subtract).then_inc(consts_dve, 1)
            eng.wait_ge(consts_dve, 4)
            eng.tensor_scalar(rate, rate, 1.0 / 8.0, None, ALU.mult).then_inc(consts_dve, 1)

        norms, shared = [], {}

        def normalise(name, src, ready, dst, banks_free, g=None, b=None, centre=True):
            def use(what, per=1):
                if what in shared:
                    shared[what] = shared[what].again()
                else:
                    shared[what] = stage("norm_" + what, per)
                return shared[what]

            before = shared.get("scaled")
            if centre:
                halves, mean, centred = use("halves_added"), use("mean"), use("centred")
            else:
                guarded = use("guarded")
            squared, squares, var = use("squared"), use("squares_added"), use("variance")
            logged, rstd, scaled = use("log_variance"), use("rstd"), use("scaled")
            done = use("affine", 2) if g is not None else scaled
            norms.append(scaled)
            body = XC if centre else src

            @part("pool")
            def _(eng):
                if before:
                    before.wait_all(eng)
                if centre:
                    with eng.Fori(0, NC) as c:
                        ready(eng, c)
                        eng.tensor_tensor(norm_sum[:, tok(c)], src[:, 0, tok(c)], src[:, 1, tok(c)],
                                          ALU.add).then_inc(halves.sem, 1)
                with eng.Fori(0, NC) as c:
                    squared.wait(eng, c)
                    if centre:
                        mean.wait(eng, c)
                    eng.tensor_tensor(norm_sum[:, tok(c)], SQ[:, 0, tok(c)], SQ[:, 1, tok(c)],
                                      ALU.add).then_inc(squares.sem, 1)

            @part("pe")
            def _(eng):
                banks_free(eng)
                eng.wait_ge(ld_mean, 16)
                if centre:
                    with eng.Fori(0, NC) as c:
                        halves.wait(eng, c)
                        eng.matmul(bank(c), mean_w, norm_sum[:, tok(c)], start=True,
                                   stop=True).then_inc(mean.sem, 1)
                with eng.Fori(0, NC) as c:
                    squares.wait(eng, c)
                    eng.matmul(bank(c + 4), mean_w, norm_sum[:, tok(c)], start=True,
                               stop=True).then_inc(var.sem, 1)

            @part("dve")
            def _(eng):
                if before:
                    before.wait_all(eng)
                if centre:
                    with eng.Fori(0, NC) as c:
                        mean.wait(eng, c)
                        ready(eng, c)
                        eng.tensor_tensor(XC[:, :, tok(c)], src[:, :, tok(c)],
                                          bank(c).broadcast_to([P, 2, CH]), ALU.subtract).then_inc(centred.sem, 1)
                else:
                    with eng.Fori(0, NC) as c:
                        var.wait(eng, c)
                        eng.tensor_scalar(norm_rstd[:, tok(c)], bank(c + 4).squeeze(1), 1e-24 / D, None,
                                          ALU.max).then_inc(guarded.sem, 1)
                with eng.Fori(0, NC) as c:
                    rstd.wait(eng, c)
                    eng.tensor_tensor(dst[:, :, tok(c)], body[:, :, tok(c)], both(norm_rstd[:, tok(c)]),
                                      ALU.mult).then_inc(scaled.sem, 1)
                    if g is not None:
                        scaled.wait(eng, c)
                        for h in range(2):
                            add = (b[:, h:h + 1], ALU.mult, ALU.add) if centre else (RMS_SCALE ** 0.5, ALU.mult, ALU.mult)
                            eng.tensor_scalar(dst[:, h, tok(c)], dst[:, h, tok(c)], g[:, h:h + 1],
                                              *add).then_inc(done.sem, 1)

            @part("act")
            def _(eng):
                if before:
                    before.wait_all(eng)
                eng.preload_act_table_set(LN_EXP)
                with eng.Fori(0, NC) as c:
                    centred.wait(eng, c) if centre else ready(eng, c)
                    eng.activation(SQ[:, :, tok(c)], body[:, :, tok(c)], ACT.Square).then_inc(squared.sem, 1)
                with eng.Fori(0, NC) as c:
                    if centre:
                        var.wait(eng, c)
                        eng.activation(norm_rstd[:, tok(c)], bank(c + 4).squeeze(1), ACT.Ln,
                                       bias=eps_col).then_inc(logged.sem, 1)
                    else:
                        guarded.wait(eng, c)
                        eng.activation(norm_rstd[:, tok(c)], norm_rstd[:, tok(c)], ACT.Ln, bias=zero_col,
                                       scale=RMS_SCALE).then_inc(logged.sem, 1)
                logged.wait_all(eng)
                with eng.Fori(0, NC) as c:
                    eng.activation(norm_rstd[:, tok(c)], norm_rstd[:, tok(c)], ACT.Exp, bias=zero_col,
                                   scale=-0.5).then_inc(rstd.sem, 1)

            return done

        def ready_of(st):
            return lambda eng, c: st.wait(eng, c)

        def all_done(*stages):
            def wait(eng):
                for st in stages:
                    st.wait_all(eng)
            return wait

        def product(eng, out, w, m, x, c, ktiles=2):
            for k in range(ktiles):
                ins = eng.matmul(out, w[:, k, m * P:(m + 1) * P], x[:, k, tok(c)], start=k == 0,
                                 stop=k == ktiles - 1)
            return ins

        def x_loaded(eng, c):
            for s in ld_x:
                eng.wait_ge(s, 16)

        ln1 = normalise("ln1", X, x_loaded, XN, lambda eng: None, vec["ln1_g"], vec["ln1_b"])

        mix = stage("mix_products", 4)
        r_out, w_exp = stage("r_copied", primed="dve"), stage("w_exponential", primed="act")
        k_sub, k_exp = stage("k_less_w", primed="dve"), stage("k_exponential")
        v_mul = stage("k_times_v", primed="dve")
        den_scan, num_scan = stage("den_scanned", 2), stage("num_scanned", 2)
        r_sig, den_ln, den_inv = stage("r_sigmoid"), stage("den_log"), stage("den_inverse")
        wkv, r_wkv = stage("wkv"), stage("r_wkv")

        @part("pe")
        def _(eng, last=norms[-1]):
            eng.wait_ge(ld_rwkv[0], 16)
            last.wait_all(eng)
            with eng.Fori(0, NC) as c:
                ln1.wait(eng, c)
                for i, (w, read) in enumerate((("Wr", r_out), ("Ww", w_exp), ("Wk", k_sub), ("Wv", v_mul))):
                    read.wait(eng, c, 0)
                    product(eng, ps[:, 2 * i, :], rwkv[w], 0, XN, c)
                    product(eng, ps[:, 2 * i + 1, :], rwkv[w], 1, XN, c).then_inc(mix.sem, 1)

        @part("act")
        def _(eng):
            with eng.Fori(0, NC) as c:
                mix.wait(eng, c, 2)
                eng.activation(B2[:, :, tok(c)], ps[:, 2:4, :], ACT.Exp, bias=zero_col).then_inc(w_exp.sem, 1)
                k_sub.wait(eng, c)
                eng.activation(B3[:, :, tok(c)], B3[:, :, tok(c)], ACT.Exp, bias=zero_col).then_inc(k_exp.sem, 1)
            eng.preload_act_table_set(SIGMOID)
            with eng.Fori(0, NC) as c:
                r_out.wait(eng, c)
                eng.activation(B1[:, :, tok(c)], B1[:, :, tok(c)], ACT.Sigmoid, bias=zero_col).then_inc(r_sig.sem, 1)
            eng.preload_act_table_set(LN_EXP)
            with eng.Fori(0, NC) as c:
                den_scan.wait(eng, c)
                num_scan.wait(eng, c)
                eng.activation(B3[:, :, tok(c)], B2[:, :, tok(c)], ACT.Ln, bias=wkv_eps_col).then_inc(den_ln.sem, 1)
            den_ln.wait_all(eng)
            with eng.Fori(0, NC) as c:
                eng.activation(B3[:, :, tok(c)], B3[:, :, tok(c)], ACT.Exp, bias=zero_col,
                               scale=-1.0).then_inc(den_inv.sem, 1)

        def scan(eng, st, coef, data, out, h, c, first):
            if first:
                start = 0.0
            else:
                st.wait(eng, c - 1)
                start = out[:, h, bass.ds(c * CH - 1, 1)]
            eng.tensor_tensor_scan(out[:, h, tok(c)], coef, data[:, h, tok(c)], start, ALU.mult,
                                   ALU.add).then_inc(st.sem, 1)

        @part("dve")
        def _(eng):
            eng.wait_ge(mask_row_out, 16)
            with eng.Fori(0, NC) as c:
                mix.wait(eng, c, 1)
                eng.tensor_copy(B1[:, :, tok(c)], ps[:, 0:2, :]).then_inc(r_out.sem, 1)
                mix.wait(eng, c, 3)
                w_exp.wait(eng, c)
                eng.tensor_tensor(B3[:, :, tok(c)], ps[:, 4:6, :], B2[:, :, tok(c)],
                                  ALU.subtract).then_inc(k_sub.sem, 1)
                mix.wait(eng, c, 4)
                k_exp.wait(eng, c)
                eng.tensor_tensor(B4[:, :, tok(c)], ps[:, 6:8, :], B3[:, :, tok(c)], ALU.mult).then_inc(v_mul.sem, 1)
            eng.wait_ge(act_const, 1)
            v_mul.wait_all(eng)

            def scans(c, first):
                for h in range(2):
                    d = decay[:, h:h + 1].broadcast_to([P, CH])
                    scan(eng, den_scan, d, B3, B2, h, c, first)
                    scan(eng, num_scan, d, B4, B5, h, c, first)

            scans(0, True)
            with eng.Fori(1, NC) as c:
                scans(c, False)
            with eng.Fori(0, NC) as c:
                den_inv.wait(eng, c)
                num_scan.wait(eng, c)
                eng.tensor_tensor(B4[:, :, tok(c)], B5[:, :, tok(c)], B3[:, :, tok(c)], ALU.mult).then_inc(wkv.sem, 1)
                wkv.wait(eng, c)
                r_sig.wait(eng, c)
                eng.tensor_tensor(XN[:, :, tok(c)], B4[:, :, tok(c)], B1[:, :, tok(c)],
                                  ALU.mult).then_inc(r_wkv.sem, 1)

        wo = stage("time_mix_out")
        x1 = stage("x_plus_time_mix")

        @part("pe")
        def _(eng):
            eng.wait_ge(ld_rwkv[1], 16)
            all_done(r_out, w_exp, k_sub, v_mul)(eng)
            with eng.Fori(0, NC) as c:
                r_wkv.wait(eng, c)
                product(eng, bank(c * 2), rwkv["Wo"], 0, XN, c)
                product(eng, bank(c * 2 + 1), rwkv["Wo"], 1, XN, c).then_inc(wo.sem, 1)

        @part("dve")
        def _(eng):
            with eng.Fori(0, NC) as c:
                wo.wait(eng, c)
                eng.tensor_tensor(B2[:, :, tok(c)], bank(c * 2, 2), X[:, :, tok(c)], ALU.add).then_inc(x1.sem, 1)

        ln2 = normalise("ln2", B2, ready_of(x1), XN, all_done(x1), vec["ln2_g"], vec["ln2_b"])
        KT = F0 // P
        key, rec, val = stage("key_products", KT), stage("receptance"), stage("channel_values", primed="pe")
        relu, squares = stage("key_relu", KT), stage("key_squared", KT)
        c_sig, c_mul = stage("receptance_sigmoid", primed="act"), stage("receptance_times_values", primed="dve")
        xx, x2 = stage("x_plus_x1"), stage("x_plus_block")
        keys = f32(work + 5 * BUF, KT, CH)

        @part("pe")
        def _(eng, last=norms[-1]):
            last.wait_all(eng)
            with eng.Fori(0, NC) as c:
                ln2.wait(eng, c)
                for j in range(KT):
                    if j >= 4:
                        relu.wait(eng, c, j - 3)
                    product(eng, ps[:, j % 4, :], rwkv["Wkey"], j, XN, c).then_inc(key.sem, 1)
                c_sig.wait(eng, c, 0)
                product(eng, ps[:, 4, :], rwkv["Wrec"], 0, XN, c)
                product(eng, ps[:, 5, :], rwkv["Wrec"], 1, XN, c).then_inc(rec.sem, 1)
                c_mul.wait(eng, c, 0)
                squares.wait(eng, c)
                for m in range(2):
                    for j in range(KT):
                        ins = eng.matmul(ps[:, 6 + m, :], rwkv["Wval"][:, j, m * P:(m + 1) * P], keys[:, j, :],
                                         start=j == 0, stop=j == KT - 1)
                ins.then_inc(val.sem, 1)

        @part("act")
        def _(eng):
            x1.wait_all(eng)
            eng.preload_act_table_set(SIGMOID)
            with eng.Fori(0, NC) as c:
                val.wait(eng, c, 0)
                for j in range(KT):
                    key.wait(eng, c, j + 1)
                    eng.activation(keys[:, j, :], ps[:, j % 4, :], ACT.Relu, bias=zero_col).then_inc(relu.sem, 1)
                rec.wait(eng, c)
                eng.activation(B4[:, :, tok(c)], ps[:, 4:6, :], ACT.Sigmoid, bias=zero_col).then_inc(c_sig.sem, 1)

        @part("pool")
        def _(eng):
            ln2.wait_all(eng)
            with eng.Fori(0, NC) as c:
                eng.tensor_tensor(B2[:, :, tok(c)], B2[:, :, tok(c)], X[:, :, tok(c)], ALU.add).then_inc(xx.sem, 1)

        @part("dve")
        def _(eng):
            with eng.Fori(0, NC) as c:
                for j in range(KT):
                    relu.wait(eng, c, j + 1)
                    eng.tensor_tensor(keys[:, j, :], keys[:, j, :], keys[:, j, :], ALU.mult).then_inc(squares.sem, 1)
                val.wait(eng, c)
                c_sig.wait(eng, c)
                eng.tensor_tensor(B1[:, :, tok(c)], ps[:, 6:8, :], B4[:, :, tok(c)], ALU.mult).then_inc(c_mul.sem, 1)
                c_mul.wait(eng, c)
                xx.wait(eng, c)
                eng.tensor_tensor(B2[:, :, tok(c)], B2[:, :, tok(c)], B1[:, :, tok(c)], ALU.add).then_inc(x2.sem, 1)

        norm0 = normalise("norm0", B2, ready_of(x2), X, all_done(c_mul, c_sig))

        def first_pass_cut(n_kt):
            return (n_kt * P, 1, 1) if n_kt * P <= CH else (n_kt * P // 4, 2, 2)

        def slots_of(n_kt):
            return NC * G * (QT * HG * first_pass_cut(n_kt)[2] + 1) + 2 * NC

        def attend(a, ready, wq, wk, wv, wo_w, ld_w, bias, banks_free, kst_free, n_kt=NKT, keep_cols=None):
            window = n_kt < NKT
            keys, kw = n_kt * P, n_kt * P // NC
            seg_keys, SIDE, ENDS = first_pass_cut(n_kt)
            PAIRS = QT * HG * ENDS
            SLOTS = 4 * (PAIRS + 1) + 2
            AT_DEN, AT_TURN, AT_INVERT, AT_OUT = (1, 1, 2, 3) if window else (2, 5, 4, 8)
            Kst_w, ctx_w, Vaug_w = Kst[:, :, 0:keys], ctxT[:, :, 0:keys], Vaug[:, 0:n_kt, :, :]
            if keep_cols is None:
                keep_cols = keep[:, a, :]
            def stage_of(name, per=1):
                key = "attn_" + name
                if a:
                    shared[key] = shared[key].again()
                elif key not in shared:
                    shared[key] = stage(key, per)
                return shared[key]

            def count(name, total):
                key = "attn_" + name
                if key not in shared:
                    shared[key] = sem(key)
                return Count(shared[key], a * total)

            k_mm, q_mm = stage_of("k_products"), stage_of("q_products")
            cuts = {}
            for s in "kq":
                cuts[s] = [stage_of(s + "_part0"), stage_of(s + "_rest1"), stage_of(s + "_part1"),
                           stage_of(s + "_part2")]
            stored = {s: [count(s + "_parts_stored0", 96), count(s + "_parts_stored1", 96)] for s in "kq"}
            v_mm, v_in = count("v_product", NKT), count("v_placed", NKT)
            v_clear, v_keep = count("v_cleared", 1), count("v_keep_column", 1)
            ld_ctx, k_rows = count("ld_context", 16), count("k_rows", 16 * (len(K_PART) + 2))
            q_const = count("q_mask_rows", 64)
            q_rows = [count(f"q_rows{i}", 4 * 96) for i in range(4)]
            max_rows = [count(f"max_rows{i}", 4 * 48) for i in range(4)]
            units = NC * G
            slots = slots_of(n_kt)
            slot_full, slot_free = count("slot_full", slots_of(NKT)), count("slot_free", slots_of(NKT))
            st_full, p_full = count("scores", units * NKT * HG), count("probabilities", units * NKT * HG)
            pv_done = count("pv_done", units * NKT)
            neg_max, max_part = count("negated_maxima", units), count("maximum_parts", 3 * units)
            o_copied, den_out, den_ln = (count(x, units) for x in ("o_copied", "denominators", "den_log"))
            den_inv, o_norm = count("den_inverse", units), count("o_normalised", units)

            @part("sync")
            def _(eng):
                kst_free(eng)
                start = 0
                if window:
                    start = eng.value_load(window_at[0:1, 1:2], min_val=0, max_val=(NKT - n_kt) * P)
                eng.dma_start(ctx_w, io["ctxT"][:, :, bass.ds(start, keys)]).then_inc(ld_ctx.sem, 16)
                for s, w, dst in (("k", kw, kparts), ("q", CH, qparts)):
                    for c in range(NC):
                        cuts[s][3].wait(eng, c)
                        for j in range(3):
                            eng.dma_start(dst[j].rearrange("(m p) t -> p m t", p=P)[:, :, c * w:(c + 1) * w],
                                          parts[:, c % 2, j, :, 0:w]).then_inc(stored[s][c % 2].sem, 16)
                    if s == "k":
                        for i in range(2):
                            stored["k"][i].wait(eng, 16 * 3 * 2)
                        for r, j in enumerate(K_PART):
                            eng.dma_start(Kst_w[DH * r:DH * (r + 1), :, :],
                                          kparts[j].rearrange("(h d) t -> d h t", d=DH)[:, :, 0:keys]).then_inc(k_rows.sem, 16)
                        mask_src = mask_rows if a == 0 else io["pad_row"]
                        if a == 0:
                            eng.wait_ge(mask_row_out, 16)
                        eng.dma_start(Kst_w[96:97, :, :], mask_src[0:1, bass.ds(start, keys)].unsqueeze(1).broadcast_to([1, H, keys]))\
                            .then_inc(k_rows.sem, 16)
                        eng.dma_start(Kst_w[97:100, :, :], io["ones"][:, 0:keys].unsqueeze(1).broadcast_to([3, H, keys]))\
                            .then_inc(k_rows.sem, 16)
                        for i in range(4):
                            eng.dma_start(Qst[96:97, i, :, :].rearrange("o h t -> o (h t)"),
                                          io["ones"][0:1, :]).then_inc(q_const.sem, 16)

            @part("pe")
            def _(eng):
                banks_free(eng)
                ld_ctx.wait(eng, 16)
                eng.wait_ge(ld_w, 16 * (1 + HG))
                with eng.Fori(0, NC) as c:
                    for m in range(2):
                        for k in range(2):
                            ins = eng.matmul(ps[:, bass.ds(c * 2 + m, 1), 0:kw], wk[:, k, m * P:(m + 1) * P],
                                             ctxT[:, k, bass.ds(c * kw, kw)], start=k == 0, stop=k == 1)
                    ins.then_inc(k_mm.sem, 1)
                with eng.Fori(0, NC) as c:
                    ready(eng, c)
                    cuts["k"][1].wait(eng, c)
                    product(eng, bank(c * 2), wq, 0, X, c)
                    product(eng, bank(c * 2 + 1), wq, 1, X, c).then_inc(q_mm.sem, 1)
                for t in range(n_kt):
                    if t == 0:
                        cuts["q"][1].wait_all(eng)
                    if t >= 4:
                        v_in.wait(eng, t - 3)
                    for k in range(2):
                        ins = eng.matmul(ps[:, t % 4, 0:D], ctxT[:, k, t * P:(t + 1) * P], wv[:, k, :],
                                         start=k == 0, stop=k == 1)
                    ins.then_inc(v_mm.sem, 1)

            def parts_ring(i, j, w):
                return parts[:, i, j, :, 0:w]

            @part("act")
            def _(eng):
                eng.preload_act_table_set(LN_EXP)
                for s, w, mm, scale in (("k", kw, k_mm, 1.0), ("q", CH, q_mm, DH ** -0.5)):
                    first, rest1, second, third = cuts[s]
                    for c in range(NC):
                        mm.wait(eng, c)
                        if c >= 2:
                            stored[s][c % 2].wait(eng, 48)
                        elif s == "q":
                            stored["k"][c % 2].wait(eng, 96)
                        eng.activation(parts_ring(c % 2, 0, w), ps[:, 2 * c:2 * c + 2, 0:w], ACT.Copy,
                                       scale=scale).then_inc(first.sem, 1)
                        rest1.wait(eng, c)
                        eng.activation(parts_ring(c % 2, 1, w), rest[:, :, 0:w], ACT.Copy).then_inc(second.sem, 1)

            @part("dve")
            def _(eng):
                for s, w, mm, scale in (("k", kw, k_mm, 1.0), ("q", CH, q_mm, DH ** -0.5)):
                    first, rest1, second, third = cuts[s]
                    for c in range(NC):
                        first.wait(eng, c)
                        if c:
                            third.wait(eng, c - 1)
                        elif s == "q":
                            cuts["k"][3].wait_all(eng)
                        eng.scalar_tensor_tensor(out=rest[:, :, 0:w], in0=ps[:, 2 * c:2 * c + 2, 0:w], scalar=scale,
                                                 in1=parts_ring(c % 2, 0, w), op0=ALU.mult,
                                                 op1=ALU.subtract).then_inc(rest1.sem, 1)
                        second.wait(eng, c)
                        eng.tensor_tensor(parts_ring(c % 2, 2, w), rest[:, :, 0:w], parts_ring(c % 2, 1, w),
                                          ALU.subtract).then_inc(third.sem, 1)

            @part("pool")
            def _(eng):
                kst_free(eng)
                eng.memset(Vaug_w, 0.0).then_inc(v_clear.sem, 1)
                v_clear.wait(eng, 1)
                eng.wait_ge(consts_dve, 5)
                if window:
                    eng.wait_ge(window_kept, 1)
                eng.tensor_copy(Vaug_w[:, :, :, DH], keep_cols.unsqueeze(2).broadcast_to([P, n_kt, H]))\
                    .then_inc(v_keep.sem, 1)

            @part("dve")
            def _(eng):
                if window:
                    first_tile = eng.value_load(window_at[0:1, 0:1], min_val=0, max_val=NKT - n_kt)
                    eng.tensor_copy(keep_cols, keep[:, 0, bass.ds(first_tile, n_kt)]).then_inc(window_kept, 1)
                    eng.wait_ge(window_kept, 1)
                v_clear.wait(eng, 1)
                for t in range(n_kt):
                    v_mm.wait(eng, t + 1)
                    eng.tensor_scalar(Vaug[:, t, :, 0:DH], ps[:, t % 4, 0:D].rearrange("p (h d) -> p h d", h=H),
                                      keep_cols[:, t:t + 1], None, ALU.mult).then_inc(v_in.sem, 1)

            def plan(u):
                first_pass = u <= 5
                pairs = [(q, h, e) for q in range(QT) for h in range(HG) for e in range(ENDS)] if first_pass else []
                taken = 0
                for kt in range(n_kt):
                    want = PAIRS * (kt + 1) // n_kt if first_pass else 0
                    mid = (taken + want) // 2
                    yield ("scores", kt, 0)
                    if kt == 0 and u > 0:
                        yield ("pv", n_kt - 1, -1)
                    yield ("scores", kt, 1)
                    for pair in pairs[taken:mid]:
                        yield ("pair",) + pair
                    yield ("scores", kt, 2)
                    yield ("scores", kt, 3)
                    for pair in pairs[mid:want]:
                        yield ("pair",) + pair
                    taken = want
                    if kt > 0:
                        yield ("pv", kt - 1, 0)
                    if kt == AT_DEN and u > 0:
                        yield ("den",)
                    if kt == AT_TURN and u < 7:
                        yield ("turn_max",)
                    if kt == AT_OUT and u == 4:
                        yield ("out", 0)
                        yield ("out", 1)

            BASE = 2 * PAIRS + 1

            def slots_before(u):
                return BASE + sum(1 for v in range(u) for s in plan(v) if s[0] in ("pair", "turn_max", "out"))

            assert slots_before(5) - slots_before(1) == SLOTS

            def unit_of(u, c):
                return 4 * c + u if 1 <= u <= 4 else (0 if u == 0 else 8 + u)

            def shift(u, c):
                return SLOTS * c if 1 <= u <= 4 else (0 if u == 0 else 2 * SLOTS)

            def chunk_of(u, c):
                return (c + u // 4) if 1 <= u <= 4 else (0 if u == 0 else 3)

            def run_units(eng, unit):
                unit(0, 0)
                with eng.Fori(0, NC - 1) as c:
                    for u in range(1, 5):
                        unit(u, c)
                for u in range(5, 8):
                    unit(u, 0)

            def slot_banks(s):
                return ps[:, 2 * (s % 2):2 * (s % 2) + 2, :]

            def score_bank(k):
                return ps[:, 4 + k % 2, :]

            def o_bank(u):
                return ps[:, 6 + u % 2, :]

            def keys_of(u, kt):
                return n_kt * u + kt

            def load_q(eng, i_ring, g, c):
                for r, j in enumerate(Q_PART):
                    eng.dma_start(Qst[DH * r:DH * (r + 1), i_ring, :, :],
                                  qparts[j].rearrange("(h d) t -> d h t", d=DH)[:, g * HG:(g + 1) * HG, tok(c)])\
                        .then_inc(q_rows[i_ring].sem, 16)

            def store_max(eng, i_ring):
                for j in range(3):
                    eng.dma_start(Qst[97 + j:98 + j, i_ring, :, :].rearrange("o h t -> o (h t)"),
                                  Mp[0:16, i_ring % 2, j, :]).then_inc(max_rows[i_ring].sem, 16)

            @part("sync")
            def _(eng):
                for i in range(2):
                    stored["q"][i].wait(eng, 16 * 3 * 2)
                for i in range(3):
                    load_q(eng, i, i, 0)
                max_part.wait(eng, 3)
                store_max(eng, 0)

                def unit(u, c):
                    i = unit_of(u, c)
                    if u > 0:
                        st_full.wait(eng, 4 * n_kt * i)
                    if u < 5:
                        v = u + 3
                        load_q(eng, v % 4, v % 4, c + v // 4 if u else 0)
                    if u < 7:
                        max_part.wait(eng, 3 * (i + 2))
                        store_max(eng, (u + 1) % 4)

                run_units(eng, unit)

            @part("pe")
            def _(eng):
                def first_pass(ring, q, h, e, s_static, s_count, skip_wait=False):
                    if not skip_wait:
                        slot_free.wait(eng, s_count - 1)
                    for x in range(SIDE):
                        seg = SIDE * e + x
                        ins = eng.matmul(slot_banks(s_static)[:, x, 0:seg_keys], Qst[0:97, ring, h, q * P:(q + 1) * P],
                                         Kst_group(ring, h)[0:97, seg * seg_keys:(seg + 1) * seg_keys], start=True, stop=True)
                    ins.then_inc(slot_full.sem, 1)

                def Kst_group(ring, h):
                    return Kst[:, ring * HG + h, :]

                def turn_max(i_par, s_static, s_count):
                    slot_free.wait(eng, s_count - 1)
                    eng.transpose(slot_banks(s_static)[0:16, 0, 0:P], Mneg[:, i_par, :], ident).then_inc(slot_full.sem, 1)

                k_rows.wait(eng, 16 * (len(K_PART) + 2))
                q_const.wait(eng, 64)
                v_in.wait(eng, n_kt)
                s = 0
                for i in range(2):
                    q_rows[i].wait(eng, 96)
                    for q in range(QT):
                        for h in range(HG):
                            for e in range(ENDS):
                                first_pass(i, q, h, e, s, s, s < 2)
                                s += 1
                    if i == 0:
                        neg_max.wait(eng, 1)
                        turn_max(0, s, s)
                        s += 1
                v_keep.wait(eng, 1)

                def unit(u, c):
                    i = unit_of(u, c)
                    s = slots_before(u)
                    par = u % 2
                    g = u % 4
                    max_rows[g].wait(eng, 48 * (chunk_of(u, c) + 1))
                    for step in plan(u):
                        what = step[0]
                        if what == "scores":
                            _, kt, h = step
                            k = 4 * kt + h
                            if u > 0 or k >= 2:
                                p_full.wait(eng, 4 * n_kt * i + k - 1)
                            eng.matmul(score_bank(k), Kst[0:ROWS, g * HG + h, kt * P:(kt + 1) * P],
                                       Qst[0:ROWS, g, h, :], start=True, stop=True).then_inc(st_full.sem, 1)
                        elif what == "pv":
                            _, kt, before = step
                            w = u + before
                            if kt == 0 and u >= 2:
                                den_ln.wait(eng, i - 1)
                            p_full.wait(eng, 4 * n_kt * (i + before) + 4 * kt + 4)
                            for h in range(HG):
                                ins = eng.matmul(o_bank(w)[32 * h:32 * h + 32, :],
                                                 Vaug[:, kt, (w % 4) * HG + h, :],
                                                 probs[:, keys_of(w, kt) % 2, h, :], start=kt == 0,
                                                 stop=kt == n_kt - 1)
                            ins.then_inc(pv_done.sem, 1)
                        elif what == "pair":
                            _, q, h, e = step
                            v = u + 2
                            if (q, h, e) == (0, 0, 0):
                                q_rows[v % 4].wait(eng, 96 * (chunk_of_next(u, c, 2) + 1))
                            first_pass(v % 4, q, h, e, s, s + shift(u, c))
                            s += 1
                        elif what == "turn_max":
                            neg_max.wait(eng, i + 2)
                            turn_max((u + 1) % 2, s, s + shift(u, c))
                            s += 1
                        elif what == "den":
                            o_copied.wait(eng, i)
                            eng.matmul(o_bank(u - 1), pick_den, Osb[:, (u - 1) % 2, :], start=True,
                                       stop=True).then_inc(den_out.sem, 1)
                        elif what == "out":
                            out(step[1], s, s + shift(u, c), i)
                            s += 1

                def out(m, s_static, s_count, units):
                    if m == 0:
                        o_norm.wait(eng, units)
                    slot_free.wait(eng, s_count - 1)
                    for g in range(G):
                        ins = eng.matmul(slot_banks(s_static)[:, 0, :], wo_w[:, g, m * P:(m + 1) * P],
                                         On[:, g, :], start=g == 0, stop=g == G - 1)
                    ins.then_inc(slot_full.sem, 1)

                run_units(eng, unit)
                p_full.wait(eng, 4 * n_kt * 16)
                for h in range(HG):
                    ins = eng.matmul(o_bank(15)[32 * h:32 * h + 32, :], Vaug[:, n_kt - 1, 3 * HG + h, :],
                                     probs[:, keys_of(7, n_kt - 1) % 2, h, :], start=False, stop=True)
                ins.then_inc(pv_done.sem, 1)
                o_copied.wait(eng, 16)
                eng.matmul(o_bank(15), pick_den, Osb[:, 1, :], start=True, stop=True).then_inc(den_out.sem, 1)
                s = slots_before(8)
                for m in range(2):
                    out(m, s + m, s + m + 2 * SLOTS, 16)

            def chunk_of_next(u, c, ahead):
                if u == 0:
                    return 0
                return c + (u + ahead) // 4 if u <= 4 else 3

            @part("act")
            def _(eng):
                def invert(u, i):
                    p = (u - 1) % 2
                    den_out.wait(eng, i)
                    eng.activation(Rden[:, p, :], o_bank(u - 1), ACT.Ln, bias=zero_col).then_inc(den_ln.sem, 1)
                    den_ln.wait(eng, i)
                    eng.activation(Rden[:, p, :], Rden[:, p, :], ACT.Exp, bias=zero_col,
                                   scale=-1.0).then_inc(den_inv.sem, 1)

                def unit(u, c):
                    i = unit_of(u, c)
                    for step in plan(u):
                        if step[0] == "scores":
                            _, kt, h = step
                            k = 4 * kt + h
                            st_full.wait(eng, 4 * n_kt * i + k + 1)
                            if h == 0 and (u > 0 or kt >= 2):
                                pv_done.wait(eng, n_kt * i + kt - 1)
                            eng.activation(probs[:, keys_of(u, kt) % 2, h, :], score_bank(k), ACT.Exp,
                                           bias=zero_col).then_inc(p_full.sem, 1)
                        if step == ("scores", AT_INVERT, 1) and u > 0:
                            invert(u, i)

                run_units(eng, unit)
                invert(16, 16)

            @part("pool")
            def _(eng):
                def normalise_o(u, c, i):
                    den_inv.wait(eng, i)
                    if u in (1, 5):
                        slot_free.wait(eng, slots_before(u) + shift(u, c))
                    eng.tensor_tensor(On[:, (u - 1) % 4, :], Osb[:, (u - 1) % 2, :], Rden[:, (u - 1) % 2, :],
                                      ALU.mult).then_inc(o_norm.sem, 1)

                def unit(u, c):
                    if u > 0:
                        normalise_o(u, c, unit_of(u, c))

                run_units(eng, unit)
                normalise_o(16, 0, 16)

            @part("dve")
            def _(eng):
                def pair(par, q, h, e, s_static, s_count):
                    slot_full.wait(eng, s_count + 1)
                    eng.tensor_reduce(MX[:, par, h * QT + q, e:e + 1], slot_banks(s_static)[:, 0:SIDE, 0:seg_keys], AX.XY,
                                      ALU.max).then_inc(slot_free.sem, 1)

                def negate(par, s_count, i):
                    slot_free.wait(eng, s_count)
                    eng.tensor_reduce(Mneg[:, par, :], MX[:, par, :, 0:ENDS], AX.X, ALU.max,
                                      negate=True).then_inc(neg_max.sem, 1)

                def cut_max(par, s_static, s_count, i):
                    src = slot_banks(s_static)[0:16, 0, 0:P]
                    slot_full.wait(eng, s_count + 1)
                    eng.tensor_copy(Mp[0:16, par, 0, :], src).then_inc(max_part.sem, 1)
                    max_part.wait(eng, 3 * i + 1)
                    eng.tensor_tensor(Mres[0:16, :], src, Mp[0:16, par, 0, :], ALU.subtract).then_inc(slot_free.sem, 1)
                    slot_free.wait(eng, s_count + 1)
                    eng.tensor_copy(Mp[0:16, par, 1, :], Mres[0:16, :]).then_inc(max_part.sem, 1)
                    max_part.wait(eng, 3 * i + 2)
                    eng.tensor_tensor(Mp[0:16, par, 2, :], Mres[0:16, :], Mp[0:16, par, 1, :],
                                      ALU.subtract).then_inc(max_part.sem, 1)

                s = 0
                for i in range(2):
                    for q in range(QT):
                        for h in range(HG):
                            for e in range(ENDS):
                                pair(i, q, h, e, s, s)
                                s += 1
                    negate(i, s, i)
                    if i == 0:
                        cut_max(0, s, s, 0)
                        s += 1

                def copy_o(u, i):
                    pv_done.wait(eng, n_kt * i)
                    if u >= 3:
                        o_norm.wait(eng, i - 2)
                    eng.tensor_copy(Osb[:, (u - 1) % 2, :], o_bank(u - 1)).then_inc(o_copied.sem, 1)

                def out(m, c, s_static, s_count):
                    slot_full.wait(eng, s_count + 1)
                    eng.scalar_tensor_tensor(out=X[:, m, tok(c)], in0=slot_banks(s_static)[:, 0, :],
                                             scalar=bias[:, m:m + 1] if bias is not None else 0.0,
                                             in1=X[:, m, tok(c)], op0=ALU.add, op1=ALU.add).then_inc(slot_free.sem, 1)

                def unit(u, c):
                    i = unit_of(u, c)
                    s = slots_before(u)
                    for step in plan(u):
                        what = step[0]
                        n = s + shift(u, c)
                        if what == "pair":
                            _, q, h, e = step
                            pair(u % 2, q, h, e, s, n)
                            s += 1
                            if (q, h, e) == (QT - 1, HG - 1, ENDS - 1):
                                negate(u % 2, n + 1, i + 2)
                        elif what == "turn_max":
                            cut_max((u + 1) % 2, s, n, i + 1)
                            s += 1
                        elif what == "out":
                            out(step[1], c, s, n)
                            s += 1
                        if step == ("pv", n_kt - 1, -1):
                            copy_o(u, i)

                run_units(eng, unit)
                copy_o(16, 16)
                s = slots_before(8)
                for m in range(2):
                    out(m, NC - 1, s + m, s + m + 2 * SLOTS)

            total = slots_before(8) + 2 * SLOTS + 2
            assert total == slots, (total, slots)

            def updated(eng, c=None):
                eng.wait_ge(slot_free.sem, (a + 1) * slots_of(NKT))

            if window:
                updated.further = {
                    "pe": [(v_mm, n_kt, NKT), (slot_full, slots, slots_of(NKT)),
                           (st_full, units * n_kt * HG, units * NKT * HG), (pv_done, units * n_kt, units * NKT)],
                    "act": [(p_full, units * n_kt * HG, units * NKT * HG)],
                    "dve": [(v_in, n_kt, NKT), (slot_free, slots, slots_of(NKT))]}
            return updated

        def one_of(narrow, wide):
            begin = {e: len(fs) for e, fs in parts_of.items()}
            ways = []
            for way in (narrow, wide):
                done = way()
                ways.append((done, {e: fs[begin[e]:] for e, fs in parts_of.items()}))
                for e, fs in parts_of.items():
                    del fs[begin[e]:]
            (narrow_done, narrow_parts), (wide_done, wide_parts) = ways

            def choose(e):
                def run(eng):
                    eng.wait_ge(window_steps, WINDOW_STEPS)
                    fits = eng.value_load(window_at[0:1, 2:3], min_val=0, max_val=1)
                    with eng.If(fits == 1):
                        for f in narrow_parts[e]:
                            f(eng)
                        for count, here, there in narrow_done.further.get(e, []):
                            count.wait(eng, here)
                            eng.sem_inc(count.sem, there - here)
                    with eng.If(fits == 0):
                        for f in wide_parts[e]:
                            f(eng)
                return run

            for e, fs in parts_of.items():
                fs.append(choose(e))
            return wide_done

        def attend0(**cut):
            return attend(0, ready_of(norm0), xatt[0]["Wq"], xatt[0]["WK"], xatt[0]["WV"], out_w[0], ld_xw[0], None,
                          all_done(norm0), all_done(norm0), **cut)

        x0_done = one_of(lambda: attend0(n_kt=WINDOW, keep_cols=window_keep), attend0)
        norm1 = normalise("norm1", X, x0_done, X, lambda eng: None)

        FK = F1 // P
        w_float = sem("ffn_weights_float")
        gu, silued, h_done = stage("gate_up", FK), stage("gate_silu", FK), stage("hidden", FK, primed="dve")
        down, x_ffn = stage("down", primed="pe"), stage("x_plus_ffn", primed="dve")
        ffn_h = f32(work + 3 * BUF, FK, CH)
        ffn_s = f32(work + 4 * BUF, 2, CH)

        @part("pool")
        def _(eng):
            eng.wait_ge(ld_ffn, 16)
            eng.tensor_copy(ffn_flat, ffn_int_flat).then_inc(w_float, 1)

        @part("pe")
        def _(eng):
            norm1.wait_all(eng)
            eng.wait_ge(w_float, 1)
            with eng.Fori(0, NC) as c:
                for j in range(FK):
                    if j >= 2:
                        h_done.wait(eng, c, j - 1)
                    product(eng, ps[:, 2 * (j % 2), :], ffn["gate"], j, X, c)
                    product(eng, ps[:, 2 * (j % 2) + 1, :], ffn["up"], j, X, c).then_inc(gu.sem, 1)
                h_done.wait(eng, c)
                x_ffn.wait(eng, c, 0)
                for m in range(2):
                    for j in range(FK):
                        ins = eng.matmul(ps[:, 4 + m, :], ffn["down"][:, j, m * P:(m + 1) * P], ffn_h[:, j, :],
                                         start=j == 0, stop=j == FK - 1)
                ins.then_inc(down.sem, 1)

        @part("act")
        def _(eng):
            eng.preload_act_table_set(SILU)
            with eng.Fori(0, NC) as c:
                for j in range(FK):
                    gu.wait(eng, c, j + 1)
                    h_done.wait(eng, c, max(j - 1, 0))
                    eng.activation(ffn_s[:, j % 2, :], ps[:, 2 * (j % 2), :], ACT.Silu, bias=zero_col,
                                   scale=DEQUANT).then_inc(silued.sem, 1)

        @part("dve")
        def _(eng):
            with eng.Fori(0, NC) as c:
                down.wait(eng, c, 0)
                for j in range(FK):
                    silued.wait(eng, c, j + 1)
                    eng.scalar_tensor_tensor(out=ffn_h[:, j, :], in0=ps[:, 2 * (j % 2) + 1, :], scalar=DEQUANT,
                                             in1=ffn_s[:, j % 2, :], op0=ALU.mult, op1=ALU.mult)\
                        .then_inc(h_done.sem, 1)
                down.wait(eng, c)
                eng.scalar_tensor_tensor(out=X[:, :, tok(c)], in0=ps[:, 4:6, :], scalar=DEQUANT,
                                         in1=X[:, :, tok(c)], op0=ALU.mult, op1=ALU.add).then_inc(x_ffn.sem, 1)

        norm2 = normalise("norm2", X, ready_of(x_ffn), X, all_done(x_ffn))

        @part("sync")
        def _(eng):
            x2.wait_all(eng)
            eng.dma_start(f32(WA, width(W_LRU)), io["w_lru"][:]).then_inc(ld_lru, 16)
            eng.dma_start(f32(xatt1_at, width(W_XATT)), io["w_xatt1"][:]).then_inc(ld_xw[1], 16)
            eng.wait_ge(consts_set, 2)
            for j in range(HG):
                eng.dma_start(out_w[1][32 * j:32 * j + DH, :, :],
                              io["w_out1"][:, j, :, :].rearrange("g i n -> i g n")).then_inc(ld_xw[1], 16)

        @part("pool")
        def _(eng):
            x2.wait_all(eng)
            eng.memset(out_w[1], 0.0).then_inc(consts_set, 1)

        rms1 = normalise("rms1", X, ready_of(norm2), XN, all_done(norm2), vec["g1"], centre=False)

        def linear(w, src, ready):
            mm = shared["linear"] = shared["linear"].again() if "linear" in shared else stage("linear_products")

            @part("pe")
            def _(eng, last=norms[-1]):
                last.wait_all(eng)
                with eng.Fori(0, NC) as c:
                    ready(eng, c)
                    product(eng, bank(c * 2), w, 0, src, c)
                    product(eng, bank(c * 2 + 1), w, 1, src, c).then_inc(mm.sem, 1)

            return mm

        @part("pe")
        def _(eng):
            eng.wait_ge(ld_lru, 16)

        lin_mm = linear(lru["W_lin"], XN, ready_of(rms1))
        lin, lin_gelu = stage("lin", 2), stage("lin_gelu")
        conv_mm = linear(lru["W_conv"], B1, lambda eng, c: (lin.wait_all(eng), None))
        conv = stage("conv", 2)

        @part("dve")
        def _(eng):
            for mm, dst, b, st in ((lin_mm, B1, "b_lin", lin), (conv_mm, B3, "b_conv", conv)):
                with eng.Fori(0, NC) as c:
                    mm.wait(eng, c)
                    for h in range(2):
                        eng.tensor_scalar(dst[:, h, tok(c)], bank(c * 2 + h).squeeze(1), vec[b][:, h:h + 1], None,
                                          ALU.add).then_inc(st.sem, 1)

        gates = stage("gate_products")
        r_gate, i_gate = stage("r_gate", 2), stage("i_gate", 2, primed="act")
        a_exp, a_sq, a_root = stage("a", 2), stage("a_squared"), stage("root")
        ix, gated, h_scan, g_out = stage("gated_input"), stage("gated"), stage("recurrence", 2), stage("gelu_times_h")

        @part("pe")
        def _(eng):
            with eng.Fori(0, NC) as c:
                conv.wait_all(eng)
                i_gate.wait(eng, c, 0)
                for m in range(2):
                    product(eng, ps[:, m, :], lru["Wa"], m, B3, c)
                for m in range(2):
                    product(eng, ps[:, 2 + m, :], lru["Wx"], m, B3, c)\
                        .then_inc(gates.sem, 1) if m else product(eng, ps[:, 2, :], lru["Wx"], 0, B3, c)

        @part("act")
        def _(eng):
            eng.preload_act_table_set(GELU)
            with eng.Fori(0, NC) as c:
                lin.wait(eng, c)
                eng.activation(B2[:, :, tok(c)], B1[:, :, tok(c)], ACT.Gelu, bias=zero_col).then_inc(lin_gelu.sem, 1)
            eng.preload_act_table_set(SIGMOID)
            with eng.Fori(0, NC) as c:
                gates.wait(eng, c)
                for h in range(2):
                    eng.activation(B4[:, h, tok(c)], ps[:, h, :], ACT.Sigmoid, bias=vec["ba"][:, h:h + 1])\
                        .then_inc(r_gate.sem, 1)
                for h in range(2):
                    eng.activation(B5[:, h, tok(c)], ps[:, 2 + h, :], ACT.Sigmoid, bias=vec["bx"][:, h:h + 1])\
                        .then_inc(i_gate.sem, 1)
            eng.wait_ge(consts_dve, 5)
            eng.preload_act_table_set(LN_EXP)
            with eng.Fori(0, NC) as c:
                r_gate.wait(eng, c)
                for h in range(2):
                    eng.activation(B4[:, h, tok(c)], B4[:, h, tok(c)], ACT.Exp, bias=zero_col,
                                   scale=rate[:, h:h + 1]).then_inc(a_exp.sem, 1)
            with eng.Fori(0, NC) as c:
                a_exp.wait(eng, c)
                eng.activation(XC[:, :, tok(c)], B4[:, :, tok(c)], ACT.Square, bias=zero_col).then_inc(a_sq.sem, 1)
            eng.preload_act_table_set(SQRT)
            a_sq.wait_all(eng)
            with eng.Fori(0, NC) as c:
                eng.activation(XC[:, :, tok(c)], XC[:, :, tok(c)], ACT.Sqrt, bias=one_col,
                               scale=-1.0).then_inc(a_root.sem, 1)

        @part("dve")
        def _(eng):
            with eng.Fori(0, NC) as c:
                i_gate.wait(eng, c)
                eng.tensor_tensor(B5[:, :, tok(c)], B5[:, :, tok(c)], B3[:, :, tok(c)], ALU.mult).then_inc(ix.sem, 1)
            with eng.Fori(0, NC) as c:
                a_root.wait(eng, c)
                ix.wait(eng, c)
                eng.tensor_tensor(XC[:, :, tok(c)], XC[:, :, tok(c)], B5[:, :, tok(c)], ALU.mult).then_inc(gated.sem, 1)
            gates.wait_all(eng)

            def scans(c, first):
                gated.wait(eng, c)
                for h in range(2):
                    scan(eng, h_scan, B4[:, h, tok(c)], XC, B3, h, c, first)

            scans(0, True)
            with eng.Fori(1, NC) as c:
                scans(c, False)
            with eng.Fori(0, NC) as c:
                h_scan.wait(eng, c)
                lin_gelu.wait(eng, c)
                eng.tensor_tensor(XN[:, :, tok(c)], B2[:, :, tok(c)], B3[:, :, tok(c)], ALU.mult).then_inc(g_out.sem, 1)

        @part("pe")
        def _(eng):
            i_gate.wait_all(eng)

        lin2_mm = linear(lru["W_lin2"], XN, ready_of(g_out))
        x_lru = stage("x_plus_recurrence", 2)

        saved, summed = stage("x_saved"), stage("x_plus_x_recurrence")

        @part("pool")
        def _(eng):
            h_scan.wait_all(eng)
            with eng.Fori(0, NC) as c:
                eng.tensor_copy(XC[:, :, tok(c)], X[:, :, tok(c)]).then_inc(saved.sem, 1)

        def add_to_x(mm, b, st, base, ready):
            @part("dve")
            def _(eng):
                with eng.Fori(0, NC) as c:
                    mm.wait(eng, c)
                    ready.wait(eng, c)
                    for h in range(2):
                        eng.scalar_tensor_tensor(out=X[:, h, tok(c)], in0=bank(c * 2 + h).squeeze(1),
                                                 scalar=vec[b][:, h:h + 1], in1=base[:, h, tok(c)], op0=ALU.add,
                                                 op1=ALU.add).then_inc(st.sem, 1)

        add_to_x(lin2_mm, "b_lin2", x_lru, X, saved)
        rms2 = normalise("rms2", X, ready_of(x_lru), XN, all_done(x_lru), vec["g2"], centre=False)

        @part("pool")
        def _(eng):
            with eng.Fori(0, NC) as c:
                x_lru.wait(eng, c)
                eng.tensor_tensor(XC[:, :, tok(c)], XC[:, :, tok(c)], X[:, :, tok(c)], ALU.add).then_inc(summed.sem, 1)

        w1_mm = linear(lru["W1"], XN, ready_of(rms2))
        m_sig, m_gelu, m_val, m_mul = stage("mlp_sigmoid", 2), stage("mlp_gelu"), stage("mlp_value", 2), stage("mlp_gated")

        @part("pe")
        def _(eng):
            m_sig.wait_all(eng)

        w2_mm = linear(lru["W2"], XN, ready_of(rms2))

        @part("act")
        def _(eng):
            eng.preload_act_table_set(SIGMOID)
            with eng.Fori(0, NC) as c:
                w1_mm.wait(eng, c)
                for h in range(2):
                    eng.activation(B1[:, h, tok(c)], bank(c * 2 + h).squeeze(1), ACT.Sigmoid,
                                   bias=vec["b1"][:, h:h + 1]).then_inc(m_sig.sem, 1)
            eng.preload_act_table_set(GELU)
            with eng.Fori(0, NC) as c:
                m_sig.wait(eng, c)
                eng.activation(B1[:, :, tok(c)], B1[:, :, tok(c)], ACT.Gelu, bias=zero_col).then_inc(m_gelu.sem, 1)

        @part("dve")
        def _(eng):
            with eng.Fori(0, NC) as c:
                w2_mm.wait(eng, c)
                for h in range(2):
                    eng.tensor_scalar(B2[:, h, tok(c)], bank(c * 2 + h).squeeze(1), vec["b2"][:, h:h + 1], None,
                                      ALU.add).then_inc(m_val.sem, 1)
            with eng.Fori(0, NC) as c:
                m_gelu.wait(eng, c)
                m_val.wait(eng, c)
                eng.tensor_tensor(B2[:, :, tok(c)], B2[:, :, tok(c)], B1[:, :, tok(c)], ALU.mult).then_inc(m_mul.sem, 1)

        @part("pe")
        def _(eng):
            m_val.wait_all(eng)

        w3_mm = linear(lru["W3"], B2, ready_of(m_mul))
        x_mlp = stage("x_plus_mlp", 2)
        add_to_x(w3_mm, "b3", x_mlp, XC, summed)
        norm3 = normalise("norm3", X, ready_of(x_mlp), X, all_done(x_mlp))

        x1_done = attend(1, ready_of(norm3), xatt[1]["Wq"], xatt[1]["WK"], xatt[1]["WV"], out_w[1], ld_xw[1],
                         vec["b_out"], all_done(norm3), all_done(norm3))
        norm4 = normalise("norm4", X, x1_done, X, lambda eng: None)

        ld_experts, ld_moe = sem("ld_experts"), sem("ld_moe_consts")
        turned, turned_out, lg_mm = sem("x_turned"), sem("x_turned_copied"), sem("logit_products")
        chain, r_exp, counted = sem("router_steps"), sem("router_exponential"), sem("experts_counted")
        scattered = sem("rows_scattered")
        rows_ld = [sem("rows_loaded0"), sem("rows_loaded1")]
        xt_mm, xt_out = sem("rows_turned"), sem("rows_turned_copied")
        e_gu, e_silu, e_h = sem("expert_gate_up"), sem("expert_silu"), sem("expert_hidden")
        th_mm, th_act, th_dve = sem("hidden_turned"), sem("hidden_copied_act"), sem("hidden_copied_dve")
        dn_mm, y_out = sem("expert_down"), sem("expert_rows_copied")
        y_stored = [sem("expert_rows_stored0"), sem("expert_rows_stored1")]
        gathered = [sem(f"rows_gathered{i}") for i in range(4)]
        out_done, stored_out = sem("out_rows"), sem("out_stored")
        var_ok, std_ok = sem("final_variance"), sem("final_std")

        def load_experts(eng, first, last):
            for e in range(first, last):
                eng.dma_start(f32(WA + e * EW, EW), io["experts_w"][e]).then_inc(ld_experts, 16)

        @part("sync")
        def _(eng):
            x1_done(eng)
            for dst, name in ((upper, "upper"), (scan_keep, "scan_keep"), (row_start, "row_start")):
                eng.dma_start(dst, io[name][:]).then_inc(ld_moe, 16)
            load_experts(eng, 0, FIRST_EXPERTS)
            norm4.wait_all(eng)
            load_experts(eng, FIRST_EXPERTS, NE)

        def run_tiles(eng, step):
            for j in range(3):
                step(j, j % 2)
            with eng.Fori(0, (TILES - 4) // 2) as m:
                for u in range(2):
                    step(m * 2 + (3 + u), (3 + u) % 2)
            step(TILES - 1, (TILES - 1) % 2)

        def first(j):
            return isinstance(j, int) and j == 0

        def early(j):
            return isinstance(j, int) and j < 2

        @part("sync")
        def _(eng):
            eng.wait_ge(scattered, 16 * 2 * NT)

            def load(j, u):
                if not early(j):
                    eng.wait_ge(xt_mm, j - 1)
                eng.dma_start(rows[:, u, :], rows_in[bass.ds(j * P, P), :]).then_inc(rows_ld[u], 16)

            def store(j, u):
                eng.wait_ge(y_out, j + 1)
                eng.dma_start(rows_out[bass.ds(j * P, P), :], y[:, u, :]).then_inc(y_stored[u], 16)

            load(0, 0)

            def step(j, u):
                if not (isinstance(j, int) and j == TILES - 1):
                    load(j + 1, 1 - u)
                if not first(j):
                    store(j - 1, 1 - u)

            run_tiles(eng, step)
            store(TILES - 1, (TILES - 1) % 2)

        @part("pe")
        def _(eng):
            norm4.wait_all(eng)
            eng.wait_ge(ld_const, 16 * N_CONST)
            for t in range(NT):
                for k in range(2):
                    ins = eng.matmul(ps[:, 0, t * NE:(t + 1) * NE], X[:, k, t * P:(t + 1) * P], router[:, k, :],
                                     start=k == 0, stop=k == 1)
            ins.then_inc(lg_mm, 1)
            for t in range(NT // 2):
                b = 1 + t % 4
                if t >= 4:
                    eng.wait_ge(turned_out, t - 3)
                for i in range(2):
                    for k in range(2):
                        ins = eng.transpose(ps[:, b, i * D + k * P:i * D + (k + 1) * P],
                                            X[:, k, (2 * t + i) * P:(2 * t + i + 1) * P], ident)
                ins.then_inc(turned, 1)
            eng.wait_ge(ld_moe, 16 * 3)
            eng.wait_ge(chain, CHAIN_CHOSEN)
            eng.matmul(ps[:, 5, 0:NT * NE], upper, chosen.rearrange("p t e -> p (t e)"), start=True, stop=True)
            eng.matmul(ps[:, 6, 0:NT * NE], mean_w, chosen.rearrange("p t e -> p (t e)"), start=True,
                       stop=True).then_inc(counted, 1)
            eng.wait_ge(turned_out, NT // 2)
            eng.wait_ge(chain, CHAIN_TABLE)
            eng.wait_ge(ld_experts, 16 * NE)

            def turn_rows(j, u):
                eng.wait_ge(rows_ld[u], j // 2 * 16 + 16 if isinstance(j, int) else (j - u) * 8 + 16)
                for k in range(2):
                    ins = eng.transpose(ps[:, 4, k * P:(k + 1) * P], rows[:, u, k * P:(k + 1) * P], ident)
                ins.then_inc(xt_mm, 1)

            def gate_up(expert, u, half):
                for w in range(2):
                    for k in range(2):
                        ins = eng.matmul(ps[:, 2 * half + w, 0:HALF], rowsT[:, u, k, :],
                                         experts_all[:, bass.ds(expert * EW + ((2 * w + k) * FE + half * HALF), HALF)],
                                         start=k == 0, stop=k == 1)
                ins.then_inc(e_gu, 1)

            def turn_hidden(u):
                for i in range(FT):
                    m = min(P, FE - i * P)
                    ins = eng.transpose(ps[0:m, 5 + i // 4, (i % 4) * P:(i % 4 + 1) * P], h_rows[:, u, i * P:i * P + m],
                                        ident)
                ins.then_inc(th_mm, 1)

            def down_product(expert):
                for i in range(FT):
                    m = min(P, FE - i * P)
                    ins = eng.matmul(ps[:, 7, 0:D], hiddenT[0:m, i, :],
                                     experts_all[0:m, bass.ds(expert * EW + (4 * FE + i * D), D)],
                                     start=i == 0, stop=i == FT - 1)
                ins.then_inc(dn_mm, 1)

            def expert_of(j):
                return eng.value_load(tile_expert[0:1, bass.ds(j, 1)], min_val=0, max_val=NE - 1)

            def finish(j, expert):
                eng.wait_ge(th_act, j + 1)
                eng.wait_ge(th_dve, j + 1)
                if not first(j):
                    eng.wait_ge(y_out, j)
                down_product(expert)

            def step(j, u):
                expert = expert_of(j)
                last_expert = None if first(j) else expert_of(j - 1)
                eng.wait_ge(xt_out, j + 1)
                if not first(j):
                    eng.wait_ge(e_h, j * 2 - 1)
                gate_up(expert, u, 0)
                if not first(j):
                    eng.wait_ge(e_h, j * 2)
                    if not early(j):
                        eng.wait_ge(th_act, j - 1)
                        eng.wait_ge(th_dve, j - 1)
                    turn_hidden(1 - u)
                gate_up(expert, u, 1)
                if not first(j):
                    finish(j - 1, last_expert)
                if not (isinstance(j, int) and j == TILES - 1):
                    turn_rows(j + 1, 1 - u)

            turn_rows(0, 0)
            run_tiles(eng, step)
            last_expert = expert_of(TILES - 1)
            eng.wait_ge(e_h, 2 * TILES)
            eng.wait_ge(th_act, TILES - 1)
            eng.wait_ge(th_dve, TILES - 1)
            turn_hidden((TILES - 1) % 2)
            finish(TILES - 1, last_expert)

        @part("act")
        def _(eng):
            eng.wait_ge(chain, CHAIN_EXP)
            eng.activation(wts[:, 1, :], wts[:, 0, :], ACT.Exp, bias=zero_col).then_inc(r_exp, 1)

            def copy_rows(j, u):
                eng.wait_ge(xt_mm, j + 1)
                if not early(j):
                    eng.wait_ge(e_gu, j * 2 - 2)
                eng.activation(rowsT[:, u, :, :], ps[:, 4, 0:2 * P].rearrange("p (k t) -> p k t", k=2),
                               ACT.Copy).then_inc(xt_out, 1)

            def silu_half(j, half):
                eng.wait_ge(e_gu, j * 2 + (half + 1))
                if not first(j):
                    eng.wait_ge(e_h, j * 2 + (half - 1))
                eng.activation(silu[:, half, :], ps[:, 2 * half, 0:HALF], ACT.Silu, bias=zero_col).then_inc(e_silu, 1)

            def copy_hidden(j):
                eng.wait_ge(th_mm, j + 1)
                if not first(j):
                    eng.wait_ge(dn_mm, j)
                eng.activation(hiddenT[:, 0:4, :], ps[:, 5, :].rearrange("p (i t) -> p i t", i=4),
                               ACT.Copy).then_inc(th_act, 1)

            eng.preload_act_table_set(SILU)
            copy_rows(0, 0)

            def step(j, u):
                silu_half(j, 0)
                if not first(j):
                    copy_hidden(j - 1)
                silu_half(j, 1)
                if not (isinstance(j, int) and j == TILES - 1):
                    copy_rows(j + 1, 1 - u)

            run_tiles(eng, step)
            copy_hidden(TILES - 1)
            for i in range(4):
                eng.wait_ge(var_ok, i + 1)
                eng.activation(std[:, 0, 4 * i:4 * i + 4], std[:, 1, 4 * i:4 * i + 4], ACT.Sqrt,
                               bias=eps_col).then_inc(std_ok, 1)

        @part("pool")
        def _(eng):
            eng.wait_ge(turned_out, NT // 2)
            eng.wait_ge(chain, CHAIN_PLACES)
            eng.wait_ge(rows_cleared, 16)
            for t in range(NT):
                for r in range(2):
                    eng.indirect_dma_start(rows_in[:, :], bass.IndirectOffsetOnAxis(ap=place[:, r, t:t + 1], axis=0),
                                           acc[:, t, :], None).then_inc(scattered, 16)
            for u in range(2):
                eng.wait_ge(y_stored[u], 16 * TILES // 2)
            for t in range(NT):
                for r in range(2):
                    eng.indirect_dma_start(back[:, r, t, :], None, rows_out[:, :],
                                           bass.IndirectOffsetOnAxis(ap=place[:, r, t:t + 1], axis=0))\
                        .then_inc(gathered[t // 4], 16)

        @part("dve")
        def _(eng):
            steps = [0]

            def step_of(ins):
                steps[0] += 1
                ins.then_inc(chain, 1)

            def link(ins):
                step_of(ins)
                eng.wait_ge(chain, steps[0])

            norm4.wait_all(eng)
            eng.wait_ge(lg_mm, 1)
            link(eng.tensor_copy(logits, ps[:, 0, 0:NT * NE].rearrange("p (t e) -> p t e", t=NT)))
            for t in range(NT):
                step_of(eng.max(top[:, t, :], logits[:, t, :]))
            eng.wait_ge(chain, steps[0])
            for t in range(NT):
                step_of(eng.max_index(top_i[:, t, :], top[:, t, :], logits[:, t, :]))
            link(eng.tensor_tensor(wts[:, 0, :], top[:, :, 1], top[:, :, 0], ALU.subtract))
            assert steps[0] == CHAIN_EXP
            link(eng.tensor_copy(top_f, top_i))
            number = experts.unsqueeze(1).broadcast_to([P, NT, NE])
            for r in range(2):
                link(eng.tensor_tensor(is_top[:, r], number, top_f[:, :, r:r + 1].broadcast_to([P, NT, NE]),
                                       ALU.is_equal))
            link(eng.tensor_tensor(chosen, is_top[:, 0], is_top[:, 1], ALU.add))
            assert steps[0] == CHAIN_CHOSEN
            for t in range(NT // 2):
                eng.wait_ge(turned, t + 1)
                eng.tensor_copy(acc[:, 2 * t:2 * t + 2, :], ps[:, 1 + t % 4, :].rearrange("p (i d) -> p i d", i=2))\
                    .then_inc(turned_out, 1)
            eng.wait_ge(ld_moe, 16 * 3)
            eng.wait_ge(counted, 1)
            link(eng.tensor_scalar(count_in, ps[:, 6, 0:NT * NE].rearrange("p (t e) -> p e t", t=NT), float(D), None,
                                   ALU.mult))
            link(eng.tensor_tensor_scan(count_to.rearrange("p e t -> p (e t)"), scan_keep,
                                        count_in.rearrange("p e t -> p (e t)"), 0.0, ALU.mult, ALU.add))
            link(eng.tensor_tensor(count_in, count_to, count_in, ALU.subtract))
            link(eng.tensor_tensor(over, count_to[:, :, NT - 1:NT].broadcast_to([P, NE, NT]),
                                   row_start[:, 0:NT].unsqueeze(1).broadcast_to([P, NE, NT]), ALU.is_gt))
            link(eng.tensor_reduce(e_rows, over, AX.X, ALU.add))
            link(eng.tensor_scalar(e_rows, e_rows, float(P), None, ALU.mult))
            link(eng.tensor_tensor_scan(e_end, scan_keep[:, 1:1 + NE], e_rows, 0.0, ALU.mult, ALU.add))
            link(eng.tensor_tensor(e_rows, e_end, e_rows, ALU.subtract))
            link(eng.tensor_tensor(count_in, count_in, e_rows.unsqueeze(2).broadcast_to([P, NE, NT]), ALU.add))
            link(eng.tensor_tensor(where, ps[:, 5, 0:NT * NE].rearrange("p (t e) -> p t e", t=NT),
                                   count_in.rearrange("p e t -> p t e"), ALU.add))
            for r in range(2):
                link(eng.tensor_tensor(is_top[:, r], is_top[:, r], where, ALU.mult))
                link(eng.tensor_reduce(place_f[:, r, :], is_top[:, r], AX.X, ALU.add))
            link(eng.tensor_copy(place, place_f))
            assert steps[0] == CHAIN_PLACES
            link(eng.tensor_tensor(ended, row_start.unsqueeze(2).broadcast_to([P, TILES, NE]),
                                   e_end.unsqueeze(1).broadcast_to([P, TILES, NE]), ALU.is_ge))
            link(eng.tensor_reduce(tile_expert_f, ended, AX.X, ALU.add))
            link(eng.tensor_scalar(tile_expert, tile_expert_f, float(NE - 1), None, ALU.min))
            assert steps[0] == CHAIN_TABLE
            eng.wait_ge(r_exp, 1)
            link(eng.tensor_scalar(wts[:, 2, :], wts[:, 1, :], 1.0, None, ALU.add))
            link(eng.reciprocal(wts[:, 2, :], wts[:, 2, :]))
            link(eng.tensor_tensor(wts[:, 3, :], wts[:, 2, :], wts[:, 1, :], ALU.mult))

            def gated_half(j, u, half):
                eng.wait_ge(e_silu, j * 2 + (half + 1))
                if half == 0 and not early(j):
                    eng.wait_ge(th_mm, j - 1)
                eng.tensor_tensor(h_rows[:, u, half * HALF:(half + 1) * HALF], ps[:, 2 * half + 1, 0:HALF],
                                  silu[:, half, :], ALU.mult).then_inc(e_h, 1)

            def copy_hidden(j):
                eng.wait_ge(th_mm, j + 1)
                if not first(j):
                    eng.wait_ge(dn_mm, j)
                eng.tensor_copy(hiddenT[:, 4, :], ps[:, 6, 0:P])
                m = FE - 5 * P
                eng.tensor_copy(hiddenT[0:m, 5, :], ps[0:m, 6, P:2 * P]).then_inc(th_dve, 1)

            def copy_y(j, u):
                eng.wait_ge(dn_mm, j + 1)
                if not early(j):
                    eng.wait_ge(y_stored[u], j // 2 * 16 if isinstance(j, int) else (j - u) * 8)
                eng.tensor_copy(y[:, u, :], ps[:, 7, 0:D]).then_inc(y_out, 1)

            def step(j, u):
                gated_half(j, u, 0)
                if not first(j):
                    copy_hidden(j - 1)
                gated_half(j, u, 1)
                if not first(j):
                    copy_y(j - 1, 1 - u)

            run_tiles(eng, step)
            copy_hidden(TILES - 1)
            copy_y(TILES - 1, (TILES - 1) % 2)

            for i in range(4):
                eng.wait_ge(gathered[i], 16 * 8)
                for t in range(4 * i, 4 * i + 4):
                    for r in range(2):
                        step_of(eng.scalar_tensor_tensor(out=acc[:, t, :], in0=back[:, r, t, :],
                                                         scalar=wts[:, 2 + r, t:t + 1], in1=acc[:, t, :],
                                                         op0=ALU.mult, op1=ALU.add))
                        eng.wait_ge(chain, steps[0])
                    step_of(eng.bn_stats(stats[:, t, :], acc[:, t, :]))
                eng.wait_ge(chain, steps[0])
                for t in range(4 * i, 4 * i + 4):
                    step_of(eng.bn_aggr(aggr[:, t, :], stats[:, t, :]))
                eng.wait_ge(chain, steps[0])
                eng.tensor_copy(std[:, 1, 4 * i:4 * i + 4], aggr[:, 4 * i:4 * i + 4, 1]).then_inc(var_ok, 1)
            for i in range(4):
                eng.wait_ge(std_ok, i + 1)
                link(eng.reciprocal(std[:, 1, 4 * i:4 * i + 4], std[:, 0, 4 * i:4 * i + 4]))
                for t in range(4 * i, 4 * i + 4):
                    eng.tensor_scalar(acc[:, t, :], acc[:, t, :], aggr[:, t, 0:1], std[:, 1, t:t + 1], ALU.subtract,
                                      ALU.mult).then_inc(out_done, 1)

        @part("sync")
        def _(eng):
            for t in range(0, NT, 4):
                eng.wait_ge(out_done, t + 4)
                eng.dma_start(io["out"][0].rearrange("(t p) d -> p t d", p=P)[:, t:t + 4, :],
                              acc[:, t:t + 4, :]).then_inc(stored_out, 16)
            eng.wait_ge(stored_out, 16 * NT // 4)

        block = ctx.enter_context(nc.Block())

        @block.sync
        def _(eng):
            for f in parts_of["sync"]:
                f(eng)

        @block.gpsimd
        def _(eng):
            for f in parts_of["pool"]:
                f(eng)

        @block.tensor
        def _(eng):
            for f in parts_of["pe"]:
                f(eng)

        @block.vector
        def _(eng):
            for f in parts_of["dve"]:
                f(eng)

        @block.scalar
        def _(eng):
            for f in parts_of["act"]:
                f(eng)


CHAIN_EXP = 2 + 2 * NT
CHAIN_CHOSEN = CHAIN_EXP + 4
CHAIN_PLACES = CHAIN_CHOSEN + 15
CHAIN_TABLE = CHAIN_PLACES + 3


def kernel(**inputs):
    import concourse.bacc as bacc
    from concourse.bass_utils import run_bass_kernel_spmd

    a = {k: np.asarray(v) for k, v in inputs.items()}

    def tiles(w, n_tiles=None):
        wt = w.T
        k = -(-wt.shape[0] // P)
        if wt.shape[0] < k * P:
            wt = np.concatenate([wt, np.zeros((k * P - wt.shape[0], wt.shape[1]), wt.dtype)])
        return wt.reshape(k, P, -1).transpose(1, 0, 2).reshape(P, -1)

    def pack(*ws):
        return np.ascontiguousarray(np.concatenate([tiles(w) for w in ws], axis=1))

    def col(v):
        return v.reshape(2, P).T

    def padded(v, n):
        return np.concatenate([v, np.zeros((n - v.shape[0],) + v.shape[1:], v.dtype)])

    l0, l1, x0, x1 = "L0_attn_", "L1_attn_", "L0_xattn_", "L1_xattn_"
    vec = [a[l0 + n] for n in VECS[:5]] + [a[l1 + n] for n in VECS[5:-1]] + [a["L1_xattn_b_out"]]
    f = np.float32
    pad = np.arange(SP) >= S
    pick = np.zeros((P, P), f)
    pick[32 * (np.arange(P) // 32) + DH, np.arange(P)] = 1.0
    arrays = {
        "xT": a["x"][0].T.reshape(2, P, T).transpose(1, 0, 2),
        "ctxT": padded(a["ctx_1024"][0], SP).T.reshape(2, P, SP).transpose(1, 0, 2),
        "mask_col": padded(a["mask_BxS2_ik0"][0].astype(np.int32), SP).reshape(NKT, P).T,
        "mask_row": padded(a["mask_BxS2_ik0"][0].astype(np.int32), SP)[None],
        "vecs": np.stack([col(v) for v in vec], axis=1),
        "mean_w": np.full((P, P), 1.0 / D, f),
        "ident": np.eye(P, dtype=f),
        "pick_den": pick,
        "pad_keep": (~pad).astype(f).reshape(NKT, P).T,
        "pad_row": np.where(pad, MASKED, 0.0).astype(f)[None].astype(mybir.dt.np(BF16)),
        "ones": np.ones((3, T), mybir.dt.np(BF16)),
        "counting": np.tile(np.arange(16, dtype=f), (P, 1)),
        "router": tiles(a["L1_ffn_w_router"]).reshape(P, 2, NE),
        "w_rwkv": pack(*[a[l0 + n] for n, _, _ in W_RWKV]),
        "w_xatt0": pack(a[x0 + "Wq"], a[x0 + "Wkv"][:D], a[x0 + "Wkv"][D:]),
        "w_out0": a[x0 + "Wo"].T.reshape(G, HG, DH, D),
        "w_ffn": pack(a["L0_ffn_w_gate"], a["L0_ffn_w_up"], a["L0_ffn_w_down"]),
        "w_lru": pack(*[a[l1 + n] for n, _, _ in W_LRU]),
        "w_xatt1": pack(a[x1 + "w_q"], a[x1 + "w_kv"][:D], a[x1 + "w_kv"][D:]),
        "w_out1": a[x1 + "w_out"].T.reshape(G, HG, DH, D),
        "upper": np.triu(np.ones((P, P), f), 1),
        "scan_keep": np.tile((np.arange(NE * NT) % NT > 0).astype(f), (P, 1)),
        "row_start": np.tile(np.arange(TILES, dtype=f) * P, (P, 1)),
        "experts_w": np.stack([pack(a["L1_ffn_w_gate"][e], a["L1_ffn_w_up"][e], a["L1_ffn_w_down"][e])
                               for e in range(NE)]),
    }
    nc = bacc.Bacc("TRN2", target_bir_lowering=False, num_devices=1)
    io, given = {}, {}
    for name, v in arrays.items():
        v = np.ascontiguousarray(v)
        given["in_" + name] = v
        io[name] = nc.dram_tensor("in_" + name, v.shape, mybir.dt.from_np(v.dtype), kind="ExternalInput").ap()
    io["out"] = nc.dram_tensor("out", (1, T, D), F32, kind="ExternalOutput").ap()
    decoder(nc, io)
    r = run_bass_kernel_spmd(nc, [given], core_ids=[0])
    return r.results[0]["out"]
```
